# Optimizing a Trainium2 kernel written in Bass

```python
import numpy as np
import jax
import jax.numpy as jnp

def _softmax(x, axis=-1):
    return jax.nn.softmax(x, axis=axis)

def _gelu(x):
    return jax.nn.gelu(x, approximate=True)

def _silu(x):
    return jax.nn.silu(x)

def _sigmoid(x):
    return jax.nn.sigmoid(x)

def _layernorm(x, axis=-1, eps=1e-05):
    m = jnp.mean(x, axis=axis, keepdims=True)
    v = jnp.var(x, axis=axis, keepdims=True)
    return (x - m) / jnp.sqrt(v + eps)

def _scatter_add(tgt, idx, src, axis=0):
    return tgt.at[idx].add(src)

def _segment_sum(src, seg, n):
    return jax.ops.segment_sum(src, seg, n)
kernel_name = 'mk_recurrent_d1_jaxref_r4_5c8bf4'

def setup_inputs(seed: int=0):
    np.random.seed(seed)
    _w = jnp.asarray

    def _L0_attn_setup():
        import jax, jax.numpy as jnp
        import numpy as np
        N_EMBD = 256
        BLOCK_SIZE = 512
        B = 8
        LN_EPS = 1e-05

        def _mlp(x, W1, b1, W2, b2):
            h = jax.nn.gelu(x @ W1 + b1, approximate=False)
            return h @ W2 + b2
        key = jax.random.key(seed)
        ks = jax.random.split(key, 14)
        C = N_EMBD
        std = 0.02
        d = {'x': jax.random.normal(ks[0], (B, BLOCK_SIZE, C), dtype=jnp.float32)}
        names = ['q', 'k', 'v']
        i = 1
        for n in names:
            d[f'W1{n}'] = jax.random.normal(ks[i], (C, C), dtype=jnp.float32) * std
            i += 1
            d[f'b1{n}'] = jnp.zeros((C,), dtype=jnp.float32)
            d[f'W2{n}'] = jax.random.normal(ks[i], (C, C), dtype=jnp.float32) * std
            i += 1
            d[f'b2{n}'] = jnp.zeros((C,), dtype=jnp.float32)
        d['ln_w'] = jnp.ones((C,), dtype=jnp.float32)
        d['ln_b'] = jnp.zeros((C,), dtype=jnp.float32)
        return d
    _L0_attn_in = _L0_attn_setup()

    def _L0_ffn_setup():
        import jax, jax.numpy as jnp
        import numpy as np
        EPS = 1e-05

        def _quantize(W):
            gamma = jnp.mean(jnp.abs(W))
            return jnp.clip(jnp.round(W / (gamma + EPS)), -1.0, 1.0)
        key = jax.random.key(seed)
        k_x, k_w1, k_b1, k_w2, k_b2 = jax.random.split(key, 5)
        n_embd = 256
        d_ff = 4 * n_embd
        B, S = (4, 1024)
        bound1 = 1.0 / np.sqrt(n_embd)
        bound2 = 1.0 / np.sqrt(d_ff)
        x = jax.random.normal(k_x, (B, S, n_embd), dtype=jnp.float32)
        W1 = jax.random.uniform(k_w1, (d_ff, n_embd), jnp.float32, -bound1, bound1)
        b1 = jax.random.uniform(k_b1, (d_ff,), jnp.float32, -bound1, bound1)
        W2 = jax.random.uniform(k_w2, (n_embd, d_ff), jnp.float32, -bound2, bound2)
        b2 = jax.random.uniform(k_b2, (n_embd,), jnp.float32, -bound2, bound2)
        return {'x': x, 'W1': W1, 'b1': b1, 'W2': W2, 'b2': b2}
    _L0_ffn_in = _L0_ffn_setup()
    _d = {'L0_attn_x': _L0_attn_in['x'], 'L0_attn_W1q': _L0_attn_in['W1q'], 'L0_attn_b1q': _L0_attn_in['b1q'], 'L0_attn_W2q': _L0_attn_in['W2q'], 'L0_attn_b2q': _L0_attn_in['b2q'], 'L0_attn_W1k': _L0_attn_in['W1k'], 'L0_attn_b1k': _L0_attn_in['b1k'], 'L0_attn_W2k': _L0_attn_in['W2k'], 'L0_attn_b2k': _L0_attn_in['b2k'], 'L0_attn_W1v': _L0_attn_in['W1v'], 'L0_attn_b1v': _L0_attn_in['b1v'], 'L0_attn_W2v': _L0_attn_in['W2v'], 'L0_attn_b2v': _L0_attn_in['b2v'], 'L0_attn_ln_w': _L0_attn_in['ln_w'], 'L0_attn_ln_b': _L0_attn_in['ln_b'], 'L0_ffn_W1': _L0_ffn_in['W1'], 'L0_ffn_b1': _L0_ffn_in['b1'], 'L0_ffn_W2': _L0_ffn_in['W2'], 'L0_ffn_b2': _L0_ffn_in['b2']}
    _x0 = _d['L0_attn_x']
    _d['L0_attn_x'] = jax.random.normal(jax.random.fold_in(jax.random.key(seed), 1), (8, 512, 256), dtype=_x0.dtype)
    del _x0
    return _d

def reference(L0_attn_x, L0_attn_W1q, L0_attn_b1q, L0_attn_W2q, L0_attn_b2q, L0_attn_W1k, L0_attn_b1k, L0_attn_W2k, L0_attn_b2k, L0_attn_W1v, L0_attn_b1v, L0_attn_W2v, L0_attn_b2v, L0_attn_ln_w, L0_attn_ln_b, L0_ffn_W1, L0_ffn_b1, L0_ffn_W2, L0_ffn_b2):

    def _L0_attn_ref(x, W1q, b1q, W2q, b2q, W1k, b1k, W2k, b2k, W1v, b1v, W2v, b2v, ln_w, ln_b):
        import jax, jax.numpy as jnp
        import numpy as np
        N_EMBD = 256
        BLOCK_SIZE = 512
        B = 8
        LN_EPS = 1e-05

        def _mlp(x, W1, b1, W2, b2):
            h = jax.nn.gelu(x @ W1 + b1, approximate=False)
            return h @ W2 + b2
        Bsz, T, C = x.shape
        q = _mlp(x, W1q, b1q, W2q, b2q)
        k = _mlp(x, W1k, b1k, W2k, b2k)
        v = _mlp(x, W1v, b1v, W2v, b2v)
        scale = np.sqrt(N_EMBD * BLOCK_SIZE).astype(np.float32)
        scores = jnp.einsum('bid,bjd->bij', q, k) / scale
        mask = jnp.tril(jnp.ones((T, T), dtype=scores.dtype))
        scores = scores * mask
        out = jnp.einsum('bij,bjd->bid', scores, v)
        mu = jnp.mean(out, axis=-1, keepdims=True)
        var = jnp.mean(jnp.square(out - mu), axis=-1, keepdims=True)
        out = (out - mu) * jax.lax.rsqrt(var + LN_EPS) * ln_w + ln_b
        return out

    def _L0_ffn_ref(x, W1, b1, W2, b2):
        import jax, jax.numpy as jnp
        import numpy as np
        EPS = 1e-05

        def _quantize(W):
            gamma = jnp.mean(jnp.abs(W))
            return jnp.clip(jnp.round(W / (gamma + EPS)), -1.0, 1.0)
        Wq1 = _quantize(W1)
        Wq2 = _quantize(W2)
        h = jax.nn.relu(jnp.einsum('bsd,fd->bsf', x, Wq1) + b1)
        out = jnp.einsum('bsf,df->bsd', h, Wq2) + b2
        return out
    x = L0_attn_x
    xn = _layernorm(x, axis=-1)
    s = _L0_attn_ref(xn, L0_attn_W1q, L0_attn_b1q, L0_attn_W2q, L0_attn_b2q, L0_attn_W1k, L0_attn_b1k, L0_attn_W2k, L0_attn_b2k, L0_attn_W1v, L0_attn_b1v, L0_attn_W2v, L0_attn_b2v, L0_attn_ln_w, L0_attn_ln_b)
    g = _silu(_L0_ffn_ref(xn, L0_ffn_W1, L0_ffn_b1, L0_ffn_W2, L0_ffn_b2))
    x = x + s * g
    return x

_drawn_inputs = setup_inputs


def setup_inputs(seed=0):
    import zlib

    import numpy as np

    out = dict(_drawn_inputs(seed))
    spreads = {'L0_attn_b1q': (0.0, 0.1),
     'L0_attn_b2q': (0.0, 0.1),
     'L0_attn_b1k': (0.0, 0.1),
     'L0_attn_b2k': (0.0, 0.1),
     'L0_attn_b1v': (0.0, 0.1),
     'L0_attn_b2v': (0.0, 0.1),
     'L0_attn_ln_w': (1.0, 0.2),
     'L0_attn_ln_b': (0.0, 0.1)}
    factors = {'L0_ffn_b1': 23.693, 'L0_ffn_b2': 64.0}
    for name, (base, spread) in spreads.items():
        noise = np.random.default_rng([zlib.crc32(name.encode()), seed]).standard_normal(out[name].shape)
        drawn = base * np.exp(spread * noise) if base else spread * noise
        out[name] = jnp.asarray(drawn.astype(out[name].dtype))
    for name, factor in factors.items():
        out[name] = (out[name] * factor).astype(out[name].dtype)
    return out
```

```python
import concourse.bass as bass
from concourse import mybir
from contextlib import ExitStack

FP32 = mybir.dt.float32
FP32R = mybir.dt.float32r
ALU = mybir.AluOpType
ACT = mybir.ActivationFunctionType

P = 128
B, T, C = 8, 512, 256
F = 4 * C
TT = T // P
CK = C // P
FT = F // P
EPS = 1e-5
INV_SCALE = 1.0 / float((C * T) ** 0.5)

LO_HI, HI_LO, HI_HI = ("lo", "hi"), ("hi", "lo"), ("hi", "hi")
FULL = (LO_HI, HI_LO, HI_HI)

AT_L1, AT_F1, AT_QK, AT_V, AT_Y0, AT_S, AT_Y1, AT_XT, AT_O = 0, 6, 14, 18, 20, 21, 25, 26, 28
FILLS, BANKS = 32, 8
S_COLS = [T - j * P for j in range(TT)]
S_AT = [sum(S_COLS[:j]) for j in range(TT)]
COL_B1, COL_B2, COL_F1 = 0, 6, 10
ROW_B2V, ROW_F2, ROW_LNW, ROW_LNB = range(4)
RING = 7


def gated_block(nc, x, w_qkv, w1t, w2t, cols, rows, out):
    ctx = ExitStack()
    with ctx:
        def sb(name, shape, dt=FP32):
            return ctx.enter_context(nc.sbuf_tensor(name, shape, dt))

        def sem(name):
            return ctx.enter_context(nc.semaphore(name))

        ident = sb("ident", [P, P])
        ones = sb("ones", [P, P])
        causal = sb("causal", [P, P])
        neg_half = sb("neg_half", [P, TT])
        col = sb("col", [P, 18])
        row = sb("row", [P, 4, C])
        w = {"hi": sb("w_hi", [P, 6, CK, C], FP32R), "lo": sb("w_lo", [P, 6, CK, C], FP32R)}
        w1q = sb("w1q", [P, CK, F], FP32R)
        w2q = sb("w2q", [P, FT, C], FP32R)
        abs_sum = sb("abs_sum", [P, 2])
        thr = sb("thr", [P, 2])
        neg_thr = sb("neg_thr", [P, 2])
        x_all = sb("x_all", [P, B, TT, C])
        xn = sb("xn", [P, TT, C])
        y = sb("y", [P, TT, C])
        gw = sb("gw", [P, TT, C])
        v32 = sb("v32", [P, TT, C])
        v = {"hi": sb("v_hi", [P, TT, C], FP32R), "lo": sb("v_lo", [P, TT, C], FP32R)}
        x_stats = sb("x_stats", [P, TT, 6])
        x_part = sb("x_part", [P, 4, TT])
        x_mean = sb("x_mean", [P, TT])
        x_var = sb("x_var", [P, TT])
        x_rstd = sb("x_rstd", [P, TT])
        o_stats = sb("o_stats", [P, TT, 6])
        o_part = sb("o_part", [P, 4, TT])
        o_mean = sb("o_mean", [P, TT])
        o_var = sb("o_var", [P, TT])
        o_rstd = sb("o_rstd", [P, TT])
        xT = {"hi": sb("xT_hi", [P, CK, T], FP32R), "lo": sb("xT_lo", [P, CK, T], FP32R)}
        act32 = sb("act32", [P, RING, T])
        g = {"hi": sb("g_hi", [P, 6, T], FP32R), "lo": sb("g_lo", [P, 6, T], FP32R)}
        r = {"hi": sb("r_hi", [P, FT, T], FP32R), "lo": sb("r_lo", [P, FT, T], FP32R)}
        qk = {"hi": sb("qk_hi", [P, 4, T], FP32R), "lo": sb("qk_lo", [P, 4, T], FP32R)}
        s32 = sb("s32", [P, sum(S_COLS)])
        s = {"hi": sb("s_hi", [P, sum(S_COLS)], FP32R), "lo": sb("s_lo", [P, sum(S_COLS)], FP32R)}
        bank = [ctx.enter_context(nc.psum_tensor(f"bank{n}", [P, T], FP32)) for n in range(BANKS)]
        raw1 = x_all[:, 3:5].rearrange("p a t c -> p (a t c)")
        raw2 = x_all[:, 1:3].rearrange("p a t c -> p (a t c)")
        raw_qkv = x_all[:, 5:8].rearrange("p a t c -> p (a t c)").rearrange("p (n k c) -> p n k c", n=6, k=CK)
        flags = act32[:, 0:2].rearrange("p a t -> p (a t)")
        abs_out = act32[:, 2:6].rearrange("p a t -> p (a t)")

        x_loaded, cols_loaded, rows_loaded = sem("x_loaded"), sem("cols_loaded"), sem("rows_loaded")
        qkv_loaded = [sem(f"qkv_loaded{n}") for n in range(6)]
        raw1_loaded, raw2_loaded = sem("raw1_loaded"), sem("raw2_loaded")
        ident_zero, consts_made, causal_filled = sem("ident_zero"), sem("consts_made"), sem("causal_filled")
        w_hi_made, w_split = sem("w_hi_made"), sem("w_split")
        w_split2 = sem("w_split2")
        abs_summed, gamma_summed, thr_made = sem("abs_summed"), sem("gamma_summed"), sem("thr_made")
        flags_made, w1_quantized, w2_quantized = sem("flags_made"), sem("w1_quantized"), sem("w2_quantized")
        x_stats_made, x_var_made, x_rstd_made, xn_made = (
            sem("x_stats_made"), sem("x_var_made"), sem("x_rstd_made"), sem("xn_made"))
        xT_summed, l1_summed, f1_summed, qk_summed, v_summed, y_summed, s_summed, o_summed = (
            sem(n) for n in ("xT_summed", "l1_summed", "f1_summed", "qk_summed", "v_summed", "y_summed",
                             "s_summed", "o_summed"))
        l1_read, f1_read, v_read, y_read, s_read, o_read = (
            sem(n) for n in ("l1_read", "f1_read", "v_read", "y_read", "s_read", "o_read"))
        xT_hi_made, xT_split = sem("xT_hi_made"), sem("xT_split")
        g_split, r_split = sem("g_split"), sem("r_split")
        qk_hi_made, qk_split = sem("qk_hi_made"), sem("qk_split")
        v_hi_made, v_split = sem("v_hi_made"), sem("v_split")
        s_hi_made, s_split = sem("s_hi_made"), sem("s_split")
        silu_made, gw_made, gb_part, gb_made = sem("silu_made"), sem("gw_made"), sem("gb_part"), sem("gb_made")
        o_stats_made, o_var_made, o_rstd_made = sem("o_stats_made"), sem("o_var_made"), sem("o_rstd_made")
        out_made, stored = sem("out_made"), sem("stored")

        def occupant(at):
            for first, n, read, before in ((AT_O, 4, o_read, 0), (AT_XT, 2, xT_split, 2), (AT_Y1, 1, y_read, 0),
                                           (AT_S, 4, s_read, 0), (AT_Y0, 1, y_read, 0), (AT_V, 2, v_read, 0),
                                           (AT_QK, 4, qk_split, 0), (AT_F1, 8, f1_read, 0), (AT_L1, 6, l1_read, 0)):
                if at >= first:
                    count = at - first + 1 + (1 if first == AT_Y1 else 0)
                    return read, (2 if read is y_read else n), count, before

        block = ctx.enter_context(nc.Block())

        @block.sync
        def _(sp):
            def load_x(b):
                sp.dma_start(x_all[:, b], x[b].rearrange("(t p) c -> p t c", p=P)).then_inc(x_loaded, 16)

            load_x(0)
            for n in range(3):
                sp.dma_start(raw_qkv[:, n], w_qkv[n].rearrange("(k p) c -> p k c", p=P)).then_inc(qkv_loaded[n], 16)
            sp.dma_start(raw1.rearrange("p (k f) -> p k f", k=CK),
                         w1t.rearrange("(k p) f -> p k f", p=P)).then_inc(raw1_loaded, 16)
            sp.dma_start(raw2.rearrange("p (f c) -> p f c", f=FT),
                         w2t.rearrange("(f p) c -> p f c", p=P)).then_inc(raw2_loaded, 16)
            for n in range(3, 6):
                sp.dma_start(raw_qkv[:, n], w_qkv[n].rearrange("(k p) c -> p k c", p=P)).then_inc(qkv_loaded[n], 16)
            sp.wait_ge(x_loaded, 16)
            sp.wait_ge(w1_quantized, 2)
            sp.wait_ge(w2_quantized, 2)
            load_x(1)
            sp.wait_ge(w_split, 3)
            sp.wait_ge(w_split2, 3)
            with sp.Fori(2, B) as b:
                sp.wait_ge(x_loaded, 16 * b)
                load_x(b)
            with sp.Fori(0, B) as b:
                sp.wait_ge(out_made, b + 1)
                sp.dma_start(out[b].rearrange("(t p) c -> p t c", p=P), x_all[:, b]).then_inc(stored, 16)
            sp.wait_ge(stored, 16 * B)

        @block.gpsimd
        def _(pool):
            nc.gpsimd.memset(ident[:], 0.0).then_inc(ident_zero, 1)
            nc.gpsimd.memset(neg_half[:], -0.5).then_inc(consts_made, 1)
            pool.wait_ge(ident_zero, 1)
            nc.gpsimd.affine_select(out=ident[:], in_=ident[:], compare_op=ALU.not_equal, fill=1.0, base=0,
                                    pattern=[[-1, P]], channel_multiplier=1).then_inc(consts_made, 1)
            nc.gpsimd.memset(ones[:], 1.0).then_inc(consts_made, 1)
            nc.gpsimd.memset(causal[:], INV_SCALE).then_inc(causal_filled, 1)
            pool.wait_ge(causal_filled, 1)
            nc.gpsimd.affine_select(out=causal[:], in_=causal[:], compare_op=ALU.is_ge, fill=0.0, base=0,
                                    pattern=[[1, P]], channel_multiplier=-1).then_inc(consts_made, 1)

            def x_rstd_of(b):
                pool.wait_ge(x_var_made, b + 1)
                nc.gpsimd.tensor_tensor(x_rstd[:], x_var[:], neg_half[:], ALU.pow).then_inc(x_rstd_made, 1)

            pool.wait_ge(consts_made, 4)
            x_rstd_of(0)
            for n in range(3, 6):
                pool.wait_ge(w_hi_made, n + 1)
                nc.gpsimd.tensor_tensor(w["lo"][:, n], raw_qkv[:, n], w["hi"][:, n].bitcast(FP32),
                                        ALU.subtract).then_inc(w_split2, 1)

            def batch(i, last=False):
                for m in range(6):
                    pool.wait_ge(l1_read, 6 * i + m + 1)
                    nc.gpsimd.tensor_tensor(g["lo"][:, m], act32[:, m], g["hi"][:, m].bitcast(FP32),
                                            ALU.subtract).then_inc(g_split, 1)
                if not last:
                    x_rstd_of(i + 1)
                pool.wait_ge(v_hi_made, i + 1)
                nc.gpsimd.tensor_tensor(v["lo"][:], v32[:], v["hi"][:].bitcast(FP32),
                                        ALU.subtract).then_inc(v_split, 1)
                pool.wait_ge(silu_made, i + 1)
                nc.gpsimd.tensor_tensor(gw[:], y[:], row[:, ROW_LNW:ROW_LNW + 1].broadcast_to((P, TT, C)),
                                        ALU.mult).then_inc(gw_made, 1)
                pool.wait_ge(o_var_made, i + 1)
                nc.gpsimd.tensor_tensor(o_rstd[:], o_var[:], neg_half[:], ALU.pow).then_inc(o_rstd_made, 1)
                pool.wait_ge(gw_made, i + 1)
                nc.gpsimd.tensor_tensor(y[:], y[:], row[:, ROW_LNB:ROW_LNB + 1].broadcast_to((P, TT, C)),
                                        ALU.mult).then_inc(gb_part, 1)
                pool.wait_ge(gb_part, i + 1)
                nc.gpsimd.tensor_tensor(x_all[:, i], x_all[:, i], y[:], ALU.add).then_inc(gb_made, 1)

            pool.wait_ge(rows_loaded, 16)
            batch(0)
            with pool.Fori(1, B - 1) as i:
                batch(i)
            batch(B - 1, last=True)

        @block.scalar
        def _(act):
            act.dma_start(col[:], cols).then_inc(cols_loaded, 16)
            act.dma_start(row[:], rows.rearrange("(o r) c -> o r c", o=1).broadcast_to((P, 4, C))).then_inc(rows_loaded, 16)

            def split_weight(n):
                act.wait_ge(qkv_loaded[n], 16)
                nc.scalar.copy(w["hi"][:, n], raw_qkv[:, n]).then_inc(w_hi_made, 1)

            def xT_hi(b):
                for k in range(CK):
                    act.wait_ge(xT_summed, 2 * b + k + 1)
                    nc.scalar.copy(xT["hi"][:, k], bank[(AT_XT + k) % BANKS][:]).then_inc(xT_hi_made, 1)

            split_weight(0)
            xT_hi(0)
            split_weight(1)
            split_weight(2)
            act.wait_ge(raw1_loaded, 16)
            nc.scalar.activation(abs_out, raw1, ACT.Abs, accum_out=abs_sum[:, 0:1]).then_inc(abs_summed, 1)
            act.wait_ge(raw2_loaded, 16)
            act.wait_ge(abs_summed, 1)
            nc.scalar.activation(abs_out, raw2, ACT.Abs, accum_out=abs_sum[:, 1:2]).then_inc(abs_summed, 1)
            for n in range(3, 6):
                split_weight(n)
            act.wait_ge(abs_summed, 2)
            act.wait_ge(w2_quantized, 2)
            act.wait_ge(cols_loaded, 16)

            def batch(i, first=False, last=False):
                for m in range(6):
                    act.wait_ge(l1_summed, 6 * i + m + 1)
                    if not first:
                        act.wait_ge(r_split, 8 * (i - 1) + m + 3 if m < 6 else 0)
                    b1 = col[:, COL_B1 + m:COL_B1 + m + 1]
                    nc.scalar.activation(g["hi"][:, m], bank[(AT_L1 + m) % BANKS][:], ACT.Gelu, bias=b1)
                    nc.scalar.activation(act32[:, m], bank[(AT_L1 + m) % BANKS][:], ACT.Gelu, bias=b1).then_inc(l1_read, 1)
                for f in range(FT):
                    slot = (6 + f) % RING
                    act.wait_ge(f1_summed, 8 * i + f + 1)
                    if f == 7:
                        act.wait_ge(r_split, 8 * i + 1)
                    elif f > 0:
                        act.wait_ge(g_split, 6 * i + f)
                    elif not first:
                        act.wait_ge(r_split, 8 * i)
                    b1 = col[:, COL_F1 + f:COL_F1 + f + 1]
                    nc.scalar.activation(r["hi"][:, f], bank[(AT_F1 + f) % BANKS][:], ACT.Relu, bias=b1)
                    nc.scalar.activation(act32[:, slot], bank[(AT_F1 + f) % BANKS][:], ACT.Relu, bias=b1).then_inc(f1_read, 1)
                for n in range(4):
                    act.wait_ge(qk_summed, 4 * i + n + 1)
                    nc.scalar.activation(qk["hi"][:, n], bank[(AT_QK + n) % BANKS][:], ACT.Identity,
                                         bias=col[:, COL_B2 + n:COL_B2 + n + 1]).then_inc(qk_hi_made, 1)
                act.wait_ge(v_read, 2 * i + 2)
                nc.scalar.copy(v["hi"][:], v32[:]).then_inc(v_hi_made, 1)
                for j in range(TT):
                    act.wait_ge(s_read, 4 * i + j + 1)
                    at = slice(S_AT[j], S_AT[j] + S_COLS[j])
                    nc.scalar.copy(s["hi"][:, at], s32[:, at]).then_inc(s_hi_made, 1)
                if not last:
                    xT_hi(i + 1)
                act.wait_ge(y_read, 2 * i + 2)
                nc.scalar.activation(y[:], y[:], ACT.Silu).then_inc(silu_made, 1)

            batch(0, first=True)
            with act.Fori(1, B - 1) as i:
                batch(i)
            batch(B - 1, last=True)

        @block.vector
        def _(dve):
            STEPS = TT + 5

            def aggregate(stats, part, mean, var, steps, before, made):
                even_mean, even_sq, odd_mean, odd_sq = (stats[:, :, n] for n in (1, 2, 4, 5))
                dve.wait_ge(steps, before + TT)
                nc.vector.tensor_tensor(part[:, 0], even_mean, odd_mean, ALU.add).then_inc(steps, 1)
                nc.vector.tensor_tensor(part[:, 1], even_mean, odd_mean, ALU.subtract).then_inc(steps, 1)
                nc.vector.scalar_tensor_tensor(part[:, 2], even_sq, C * EPS, odd_sq, ALU.add, ALU.add).then_inc(steps, 1)
                dve.wait_ge(steps, before + TT + 3)
                nc.vector.tensor_scalar(mean[:], part[:, 0], 0.5, None, ALU.mult).then_inc(steps, 1)
                nc.vector.scalar_tensor_tensor(part[:, 3], part[:, 1], 0.25, part[:, 1], ALU.mult, ALU.mult).then_inc(steps, 1)
                dve.wait_ge(steps, before + TT + 5)
                nc.vector.scalar_tensor_tensor(var[:], part[:, 2], 1.0 / C, part[:, 3], ALU.mult, ALU.add).then_inc(made, 1)

            def x_statistics(b):
                dve.wait_ge(x_loaded, 16 * b + 16)
                for t in range(TT):
                    nc.vector.bn_stats(x_stats[:, t], x_all[:, b, t]).then_inc(x_stats_made, 1)
                aggregate(x_stats, x_part, x_mean, x_var, x_stats_made, STEPS * b, x_var_made)

            def x_normalise(b):
                dve.wait_ge(x_rstd_made, b + 1)
                for t in range(TT):
                    nc.vector.tensor_scalar(xn[:, t], x_all[:, b, t], x_mean[:, t:t + 1], x_rstd[:, t:t + 1],
                                            ALU.subtract, ALU.mult).then_inc(xn_made, 1)

            def xT_lo(b):
                for k in range(CK):
                    dve.wait_ge(xT_hi_made, 2 * b + k + 1)
                    nc.vector.tensor_tensor(xT["lo"][:, k], bank[(AT_XT + k) % BANKS][:],
                                            xT["hi"][:, k].bitcast(FP32), ALU.subtract).then_inc(xT_split, 1)

            x_statistics(0)
            x_normalise(0)

            def split_weight(n):
                dve.wait_ge(w_hi_made, n + 1)
                nc.vector.tensor_tensor(w["lo"][:, n], raw_qkv[:, n], w["hi"][:, n].bitcast(FP32),
                                        ALU.subtract).then_inc(w_split, 1)

            split_weight(0)
            xT_lo(0)
            split_weight(1)
            split_weight(2)
            for n, raw, quant, done in ((0, raw1, w1q[:].rearrange("p a b -> p (a b)"), w1_quantized),
                                        (1, raw2, w2q[:].rearrange("p a b -> p (a b)"), w2_quantized)):
                dve.wait_ge(gamma_summed, n + 1)
                total = bank[6 + n][:, 0:1]
                nc.vector.tensor_scalar(thr[:, n:n + 1], total, 0.5 / (C * F), 0.5 * EPS,
                                        ALU.mult, ALU.add).then_inc(thr_made, 1)
                nc.vector.tensor_scalar(neg_thr[:, n:n + 1], total, -0.5 / (C * F), -0.5 * EPS,
                                        ALU.mult, ALU.add).then_inc(thr_made, 1)
                dve.wait_ge(thr_made, 2 * n + 2)
                for h in range(2):
                    part = slice(h * F, (h + 1) * F)
                    if n or h:
                        dve.wait_ge(done if h else w1_quantized, 1 if h else 2)
                    nc.vector.tensor_scalar(flags, raw[:, part], neg_thr[:, n:n + 1], None,
                                            ALU.is_lt).then_inc(flags_made, 1)
                    dve.wait_ge(flags_made, 2 * n + h + 1)
                    nc.vector.scalar_tensor_tensor(quant[:, part], raw[:, part], thr[:, n:n + 1], flags,
                                                   ALU.is_gt, ALU.subtract).then_inc(done, 1)
            dve.wait_ge(rows_loaded, 16)
            dve.wait_ge(cols_loaded, 16)
            dve.wait_ge(consts_made, 4)

            def batch(i, last=False):
                if not last:
                    x_statistics(i + 1)
                for f in range(FT):
                    dve.wait_ge(f1_read, 8 * i + f + 1)
                    nc.vector.tensor_tensor(r["lo"][:, f], act32[:, (6 + f) % RING], r["hi"][:, f].bitcast(FP32),
                                            ALU.subtract).then_inc(r_split, 1)
                if not last:
                    x_normalise(i + 1)
                for n in range(4):
                    dve.wait_ge(qk_hi_made, 4 * i + n + 1)
                    nc.vector.scalar_tensor_tensor(qk["lo"][:, n], bank[(AT_QK + n) % BANKS][:],
                                                   col[:, COL_B2 + n:COL_B2 + n + 1], qk["hi"][:, n].bitcast(FP32),
                                                   ALU.add, ALU.subtract).then_inc(qk_split, 1)

                def add_row(dst, at, n, which, read):
                    nc.vector.tensor_tensor(dst[:, 2 * n:2 * n + 2], bank[at % BANKS][:].rearrange("p (t c) -> p t c", t=2),
                                            row[:, which:which + 1].broadcast_to((P, 2, C)), ALU.add).then_inc(read, 1)

                for n in range(2):
                    dve.wait_ge(v_summed, 2 * i + n + 1)
                    add_row(v32, AT_V + n, n, ROW_B2V, v_read)
                dve.wait_ge(y_summed, 2 * i + 1)
                add_row(y, AT_Y0, 0, ROW_F2, y_read)

                def s_scale(j):
                    dve.wait_ge(s_summed, 4 * i + j + 1)
                    src = bank[(AT_S + j) % BANKS]
                    last_op = nc.vector.tensor_tensor(s32[:, S_AT[j]:S_AT[j] + P], src[:, 0:P], causal[:], ALU.mult)
                    if S_COLS[j] > P:
                        last_op = nc.vector.tensor_scalar(s32[:, S_AT[j] + P:S_AT[j] + S_COLS[j]], src[:, P:S_COLS[j]],
                                                          INV_SCALE, None, ALU.mult)
                    last_op.then_inc(s_read, 1)

                def s_lo(j):
                    dve.wait_ge(s_hi_made, 4 * i + j + 1)
                    at = slice(S_AT[j], S_AT[j] + S_COLS[j])
                    nc.vector.tensor_tensor(s["lo"][:, at], s32[:, at], s["hi"][:, at].bitcast(FP32),
                                            ALU.subtract).then_inc(s_split, 1)

                s_scale(0)
                for j in range(1, TT):
                    s_scale(j)
                    s_lo(j - 1)
                s_lo(TT - 1)
                dve.wait_ge(y_summed, 2 * i + 2)
                add_row(y, AT_Y1, 1, ROW_F2, y_read)
                if not last:
                    xT_lo(i + 1)
                for t in range(TT):
                    dve.wait_ge(o_summed, 4 * i + t + 1)
                    nc.vector.bn_stats(o_stats[:, t], bank[(AT_O + t) % BANKS][:, 0:C]).then_inc(o_stats_made, 1)
                aggregate(o_stats, o_part, o_mean, o_var, o_stats_made, STEPS * i, o_var_made)
                dve.wait_ge(gb_part, i + 1)
                for t in range(TT):
                    nc.vector.scalar_tensor_tensor(gw[:, t], bank[(AT_O + t) % BANKS][:, 0:C], o_mean[:, t:t + 1], gw[:, t],
                                                   ALU.subtract, ALU.mult).then_inc(o_read, 1)
                dve.wait_ge(o_rstd_made, i + 1)
                dve.wait_ge(gb_made, i + 1)
                dve.wait_ge(o_read, 4 * i + 4)
                for t in range(TT):
                    last_op = nc.vector.scalar_tensor_tensor(x_all[:, i, t], gw[:, t], o_rstd[:, t:t + 1], x_all[:, i, t],
                                                             ALU.mult, ALU.add)
                last_op.then_inc(out_made, 1)

            batch(0)
            with dve.Fori(1, B - 1) as i:
                batch(i)
            batch(B - 1, last=True)

        @block.tensor
        def _(pe):
            def claim(i, at, first=False):
                read, per_batch, count, before = occupant((at - BANKS) % FILLS)
                if at >= BANKS:
                    pe.wait_ge(read, per_batch * i + count + before)
                elif not first:
                    pe.wait_ge(read, per_batch * (i - 1) + count + before)
                elif before:
                    pe.wait_ge(read, at - (AT_XT % BANKS) + 1)
                return bank[at % BANKS]

            def transpose_x(i, b, first=False):
                for k in range(CK):
                    dst = bank[(AT_XT + k) % BANKS] if first else claim(i, AT_XT + k)
                    pe.wait_ge(xn_made, 4 * b + 4)
                    for t in range(TT):
                        last = nc.tensor.transpose(dst[:, t * P:(t + 1) * P], xn[:, t, k * P:(k + 1) * P], ident[:])
                    last.then_inc(xT_summed, 1)

            pe.wait_ge(consts_made, 4)
            transpose_x(0, 0, first=True)

            def split_product(dst, pairs):
                for n, (a, b) in enumerate(pairs):
                    last = nc.tensor.matmul(dst, a, b, start=(n == 0), stop=(n == len(pairs) - 1))
                return last

            def ffn_out(i, n):
                dst = claim(i, (AT_Y0, AT_Y1)[n])
                for t in (2 * n, 2 * n + 1):
                    last = split_product(dst[:, (t % 2) * C:(t % 2 + 1) * C],
                                         [(r[part][:, f, t * P:(t + 1) * P], w2q[:, f])
                                          for part in ("lo", "hi") for f in range(FT)])
                last.then_inc(y_summed, 1)

            def batch(i, first=False, last=False):
                pe.wait_ge(xT_split, 2 * i + 2)
                for m in range(6):
                    if first:
                        pe.wait_ge(w_split, m // 2 + 1)
                    dst = claim(i, AT_L1 + m, first)
                    h = slice((m % 2) * P, (m % 2 + 1) * P)
                    split_product(dst[:], [(w[a][:, m // 2, k, h], xT[b][:, k])
                                           for a, b in FULL for k in range(CK)]).then_inc(l1_summed, 1)
                if first:
                    for n in range(2):
                        pe.wait_ge(abs_summed, n + 1)
                        nc.tensor.matmul(bank[6 + n][:, 0:1], ones[:], abs_sum[:, n:n + 1],
                                         start=True, stop=True).then_inc(gamma_summed, 1)
                    pe.wait_ge(w1_quantized, 2)
                for f in range(FT):
                    if first and f == 1:
                        pe.wait_ge(thr_made, 4)
                    dst = claim(i, AT_F1 + f, first)
                    split_product(dst[:], [(w1q[:, k, f * P:(f + 1) * P], xT[part][:, k])
                                           for part in ("lo", "hi") for k in range(CK)]).then_inc(f1_summed, 1)
                if first:
                    pe.wait_ge(w_split2, 3)
                for n in range(4):
                    pe.wait_ge(g_split, 6 * i + 2 * (n // 2) + 2)
                    dst = claim(i, AT_QK + n)
                    h = slice((n % 2) * P, (n % 2 + 1) * P)
                    split_product(dst[:], [(w[a][:, 3 + n // 2, k, h], g[b][:, 2 * (n // 2) + k])
                                           for a, b in FULL for k in range(CK)]).then_inc(qk_summed, 1)
                pe.wait_ge(g_split, 6 * i + 6)
                for n in range(2):
                    dst = claim(i, AT_V + n)
                    for t in (2 * n, 2 * n + 1):
                        done = split_product(dst[:, (t % 2) * C:(t % 2 + 1) * C],
                                             [(g[a][:, 4 + k, t * P:(t + 1) * P], w[b][:, 5, k])
                                              for a, b in FULL for k in range(CK)])
                    done.then_inc(v_summed, 1)
                pe.wait_ge(r_split, 8 * i + 8)
                if first:
                    pe.wait_ge(w2_quantized, 2)
                ffn_out(i, 0)
                pe.wait_ge(qk_split, 4 * i + 4)
                for j in range(TT):
                    dst = claim(i, AT_S + j)
                    split_product(dst[:, 0:S_COLS[j]], [(qk[a][:, 2 + k, j * P:(j + 1) * P], qk[b][:, k, j * P:T])
                                                        for a, b in FULL for k in range(CK)]).then_inc(s_summed, 1)
                ffn_out(i, 1)
                if not last:
                    transpose_x(i, i + 1)
                pe.wait_ge(v_split, i + 1)
                for t in range(TT):
                    pe.wait_ge(s_split, 4 * i + t + 1)
                    dst = claim(i, AT_O + t)
                    split_product(dst[:, 0:C], [(s[a][:, S_AT[j] + (t - j) * P:S_AT[j] + (t - j + 1) * P], v[b][:, j])
                                                for a, b in FULL for j in range(t + 1)]).then_inc(o_summed, 1)

            batch(0, first=True)
            with pe.Fori(1, B - 1) as i:
                batch(i)
            batch(B - 1, last=True)


def kernel(**inputs):
    import numpy as np
    import concourse.bacc as bacc
    from concourse.bass_utils import run_bass_kernel_spmd

    def by_partition(name):
        return np.asarray(inputs[name]).reshape(-1, P).T

    arrays = {"x": np.ascontiguousarray(inputs["L0_attn_x"])}
    for name in ("W1q", "W1k", "W1v", "W2q", "W2k", "W2v"):
        arrays[name] = np.ascontiguousarray(inputs["L0_attn_" + name])
    arrays["w1t"] = np.ascontiguousarray(np.asarray(inputs["L0_ffn_W1"]).T)
    arrays["w2t"] = np.ascontiguousarray(np.asarray(inputs["L0_ffn_W2"]).T)
    arrays["cols"] = np.ascontiguousarray(np.concatenate(
        [by_partition(n) for n in ("L0_attn_b1q", "L0_attn_b1k", "L0_attn_b1v", "L0_attn_b2q", "L0_attn_b2k",
                                   "L0_ffn_b1")], axis=1))
    arrays["rows"] = np.ascontiguousarray(np.stack(
        [np.asarray(inputs[n]) for n in ("L0_attn_b2v", "L0_ffn_b2", "L0_attn_ln_w", "L0_attn_ln_b")]))

    nc = bacc.Bacc("TRN2", target_bir_lowering=False, num_devices=1, dynamic_dma_scratch_size=1024)
    aps = {n: nc.dram_tensor(f"in_{n}", a.shape, FP32, kind="ExternalInput").ap() for n, a in arrays.items()}
    out = nc.dram_tensor("out", (B, T, C), FP32, kind="ExternalOutput").ap()
    gated_block(nc, aps["x"], [aps[n] for n in ("W1q", "W1k", "W1v", "W2q", "W2k", "W2v")],
                aps["w1t"], aps["w2t"], aps["cols"], aps["rows"], out)
    result = run_bass_kernel_spmd(nc, [{f"in_{n}": a for n, a in arrays.items()}], core_ids=[0])
    return result.results[0]["out"]
```

```python
import concourse.bass as bass
from concourse import mybir
from contextlib import ExitStack

FP32 = mybir.dt.float32
FP32R = mybir.dt.float32r
ALU = mybir.AluOpType
ACT = mybir.ActivationFunctionType

P = 128
B, T, C = 8, 512, 256
F = 4 * C
TT = T // P
CK = C // P
FT = F // P
EPS = 1e-5
INV_SCALE = 1.0 / float((C * T) ** 0.5)

LO_HI, HI_LO, HI_HI = ("lo", "hi"), ("hi", "lo"), ("hi", "hi")
FULL = (LO_HI, HI_LO, HI_HI)

AT_L1, AT_F1, AT_K, AT_D, AT_V, AT_Y0, AT_S, AT_Y1, AT_XT, AT_O = 0, 6, 14, 16, 17, 19, 20, 24, 26, 28
FILLS, BANKS = 32, 8
S_COLS = [T - j * P for j in range(TT)]
S_AT = [sum(S_COLS[:j]) for j in range(TT)]
COL_B1, COL_B2, COL_F1 = 0, 6, 10
ROW_B2V, ROW_F2, ROW_LNW, ROW_LNB = range(4)
WARM_UP = 14
RING = 7


def gated_block(nc, x, w_qkv, w1t, w2t, cols, rows, out):
    ctx = ExitStack()
    with ctx:
        def sb(name, shape, dt=FP32):
            return ctx.enter_context(nc.sbuf_tensor(name, shape, dt))

        def sem(name):
            return ctx.enter_context(nc.semaphore(name))

        ident = sb("ident", [P, P])
        ones = sb("ones", [P, P])
        causal = sb("causal", [P, P])
        neg_half = sb("neg_half", [P, TT])
        col = sb("col", [P, 18])
        row = sb("row", [P, 4, C])
        w = {"hi": sb("w_hi", [P, 5, CK, C], FP32R), "lo": sb("w_lo", [P, 5, CK, C], FP32R)}
        z_bias = sb("z_bias", [P, CK])
        d_weight = sb("d_weight", [P, CK, 2], FP32R)
        d_const = sb("d_const", [P, 1])
        w1q = sb("w1q", [P, CK, F], FP32R)
        w2q = sb("w2q", [P, FT, C], FP32R)
        abs_sum = sb("abs_sum", [P, 2])
        thr = sb("thr", [P, 2])
        neg_thr = sb("neg_thr", [P, 2])
        x_all = sb("x_all", [P, B, TT, C])
        xn = sb("xn", [P, TT, C])
        y = sb("y", [P, TT, C])
        gw = sb("gw", [P, TT, C])
        v32 = sb("v32", [P, TT, C])
        v = {"hi": sb("v_hi", [P, TT, C], FP32R), "lo": sb("v_lo", [P, TT, C], FP32R)}
        x_stats = sb("x_stats", [P, TT, 6])
        x_part = sb("x_part", [P, 4, TT])
        x_mean = sb("x_mean", [P, TT])
        x_var = sb("x_var", [P, TT])
        x_rstd = sb("x_rstd", [P, TT])
        o_stats = sb("o_stats", [P, TT, 6])
        o_part = sb("o_part", [P, 4, TT])
        o_mean = sb("o_mean", [P, TT])
        o_var = sb("o_var", [P, TT])
        o_rstd = sb("o_rstd", [P, TT])
        xT = {"hi": sb("xT_hi", [P, CK, T], FP32R), "lo": sb("xT_lo", [P, CK, T], FP32R)}
        act32 = sb("act32", [P, RING, T])
        g = {"hi": sb("g_hi", [P, 6, T], FP32R), "lo": sb("g_lo", [P, 6, T], FP32R)}
        r = {"hi": sb("r_hi", [P, FT, T], FP32R), "lo": sb("r_lo", [P, FT, T], FP32R)}
        z = {"hi": sb("z_hi", [P, CK, T], FP32R), "lo": sb("z_lo", [P, CK, T], FP32R)}
        d_sum = sb("d_sum", [P, TT])
        d = sb("d", [P, TT])
        s32 = sb("s32", [P, sum(S_COLS)])
        s = {"hi": sb("s_hi", [P, sum(S_COLS)], FP32R), "lo": sb("s_lo", [P, sum(S_COLS)], FP32R)}
        bank = [ctx.enter_context(nc.psum_tensor(f"bank{n}", [P, T], FP32)) for n in range(BANKS)]
        raw1 = x_all[:, 3:5].rearrange("p a t c -> p (a t c)")
        raw2 = x_all[:, 1:3].rearrange("p a t c -> p (a t c)")
        raw_qkv = x_all[:, 5:8].rearrange("p a t c -> p (a t c)").rearrange("p (n k c) -> p n k c", n=6, k=CK)
        flags = s32[:, 0:F]
        abs_out = r["lo"][:, 0:4].rearrange("p a t -> p (a t)")

        x0_loaded = [sem(f"x0_loaded{h}") for h in range(2)]
        x_loaded, cols_loaded, rows_loaded = sem("x_loaded"), sem("cols_loaded"), sem("rows_loaded")
        qkv_loaded = [sem(f"qkv_loaded{n}") for n in range(6)]
        raw1_loaded, raw2_loaded = sem("raw1_loaded"), sem("raw2_loaded")
        ident_zero, consts_made, causal_filled = sem("ident_zero"), sem("consts_made"), sem("causal_filled")
        w_hi_made, w_split, w2v_split = sem("w_hi_made"), sem("w_split"), sem("w2v_split")
        folded, fold_hi_made, fold_read = sem("folded"), sem("fold_hi_made"), sem("fold_read")
        abs_summed, gamma_summed, thr_made = sem("abs_summed"), sem("gamma_summed"), sem("thr_made")
        flags_made, w1_quantized, w2_quantized = sem("flags_made"), sem("w1_quantized"), sem("w2_quantized")
        x_stats_made, x_var_made, x_rstd_made, xn_made = (
            sem("x_stats_made"), sem("x_var_made"), sem("x_rstd_made"), sem("xn_made"))
        xT_summed, l1_summed, f1_summed, z_summed, d_summed, v_summed, y_summed, s_summed, o_summed = (
            sem(n) for n in ("xT_summed", "l1_summed", "f1_summed", "z_summed", "d_summed", "v_summed", "y_summed",
                             "s_summed", "o_summed"))
        l1_read, f1_read, d_read, v_read, y_read, s_read, o_read = (
            sem(n) for n in ("l1_read", "f1_read", "d_read", "v_read", "y_read", "s_read", "o_read"))
        xT_hi_made, xT_split = sem("xT_hi_made"), sem("xT_split")
        g_split, r_split = sem("g_split"), sem("r_split")
        z_hi_made, z_split, d_made = sem("z_hi_made"), sem("z_split"), sem("d_made")
        v_hi_made, v_split = sem("v_hi_made"), sem("v_split")
        s_hi_made, s_split = sem("s_hi_made"), sem("s_split")
        silu_made, gw_made, gb_part, gb_made = sem("silu_made"), sem("gw_made"), sem("gb_part"), sem("gb_made")
        o_stats_made, o_var_made, o_rstd_made = sem("o_stats_made"), sem("o_var_made"), sem("o_rstd_made")
        out_made, stored = sem("out_made"), sem("stored")

        STAGES = ((AT_L1, 6, l1_read, 6, 0), (AT_F1, FT, f1_read, FT, 0), (AT_K, 2, z_split, 2, 0),
                  (AT_D, 1, d_read, 1, 0), (AT_V, 2, v_read, 2, 0), (AT_Y0, 1, y_read, 3, 0),
                  (AT_S, TT, s_read, TT, 0), (AT_Y1, 2, y_read, 3, 1), (AT_XT, CK, xT_split, CK, CK),
                  (AT_O, TT, o_read, TT, 0))

        def reading_of(at):
            for first, fills, read, per_batch, before in STAGES:
                if first <= at < first + fills:
                    return read, per_batch, before + at - first + 1

        block = ctx.enter_context(nc.Block())

        @block.sync
        def _(sp):
            def load_x(b):
                sp.dma_start(x_all[:, b], x[b].rearrange("(t p) c -> p t c", p=P)).then_inc(x_loaded, 16)

            def load_square(n):
                sp.dma_start(raw_qkv[:, n], w_qkv[n].rearrange("(k p) c -> p k c", p=P)).then_inc(qkv_loaded[n], 16)

            sp.dma_start(x_all[:, 0, 0:2], x[0, 0:2 * P].rearrange("(t p) c -> p t c", p=P)).then_inc(x0_loaded[0], 16)
            load_square(0)
            load_square(1)
            sp.dma_start(raw1.rearrange("p (k f) -> p k f", k=CK),
                         w1t.rearrange("(k p) f -> p k f", p=P)).then_inc(raw1_loaded, 16)
            load_square(2)
            sp.dma_start(raw2.rearrange("p (f c) -> p f c", f=FT),
                         w2t.rearrange("(f p) c -> p f c", p=P)).then_inc(raw2_loaded, 16)
            for n in range(3, 6):
                load_square(n)
            sp.wait_ge(w1_quantized, 2)
            sp.wait_ge(w2_quantized, 2)
            load_x(1)
            sp.wait_ge(w_split, 3)
            sp.wait_ge(w2v_split, 1)
            sp.wait_ge(folded, 2)
            with sp.Fori(2, B) as b:
                sp.wait_ge(x_loaded, 16 * b - 16)
                load_x(b)
            with sp.Fori(0, B) as b:
                for h in range(2):
                    sp.wait_ge(out_made, 2 * b + h + 1)
                    sp.dma_start(out[b, h * 2 * P:(h + 1) * 2 * P].rearrange("(t p) c -> p t c", p=P),
                                 x_all[:, b, 2 * h:2 * h + 2]).then_inc(stored, 16)
            sp.wait_ge(stored, 2 * 16 * B)

        @block.gpsimd
        def _(pool):
            nc.gpsimd.memset(ident[:], 0.0).then_inc(ident_zero, 1)
            nc.gpsimd.memset(neg_half[:], -0.5).then_inc(consts_made, 1)
            pool.wait_ge(ident_zero, 1)
            nc.gpsimd.affine_select(out=ident[:], in_=ident[:], compare_op=ALU.not_equal, fill=1.0, base=0,
                                    pattern=[[-1, P]], channel_multiplier=1).then_inc(consts_made, 1)
            nc.gpsimd.memset(ones[:], 1.0).then_inc(consts_made, 1)
            nc.gpsimd.memset(causal[:], INV_SCALE).then_inc(causal_filled, 1)
            pool.wait_ge(causal_filled, 1)
            nc.gpsimd.affine_select(out=causal[:], in_=causal[:], compare_op=ALU.is_ge, fill=0.0, base=0,
                                    pattern=[[1, P]], channel_multiplier=-1).then_inc(consts_made, 1)

            def x_rstd_of(b):
                pool.wait_ge(x_var_made, b + 1)
                nc.gpsimd.tensor_tensor(x_rstd[:], x_var[:], neg_half[:], ALU.pow).then_inc(x_rstd_made, 1)

            pool.wait_ge(consts_made, 4)
            x_rstd_of(0)
            pool.wait_ge(w_hi_made, 4)
            nc.gpsimd.tensor_tensor(w["lo"][:, 4], raw_qkv[:, 5], w["hi"][:, 4].bitcast(FP32),
                                    ALU.subtract).then_inc(w2v_split, 1)

            def batch(i, last=False):
                for m in range(6):
                    pool.wait_ge(l1_read, 6 * i + m + 1)
                    nc.gpsimd.tensor_tensor(g["lo"][:, m], act32[:, m], g["hi"][:, m].bitcast(FP32),
                                            ALU.subtract).then_inc(g_split, 1)
                if not last:
                    x_rstd_of(i + 1)
                pool.wait_ge(v_hi_made, i + 1)
                nc.gpsimd.tensor_tensor(v["lo"][:], v32[:], v["hi"][:].bitcast(FP32),
                                        ALU.subtract).then_inc(v_split, 1)

                def offset(h):
                    half = slice(2 * h, 2 * h + 2)
                    pool.wait_ge(gw_made, 2 * i + h + 1)
                    nc.gpsimd.tensor_tensor(y[:, half], y[:, half], row[:, ROW_LNB:ROW_LNB + 1].broadcast_to((P, 2, C)),
                                            ALU.mult).then_inc(gb_part, 1)
                    pool.wait_ge(gb_part, 2 * i + h + 1)
                    nc.gpsimd.tensor_tensor(x_all[:, i, half], x_all[:, i, half], y[:, half],
                                            ALU.add).then_inc(gb_made, 1)

                def o_rstd_of(h):
                    half = slice(2 * h, 2 * h + 2)
                    pool.wait_ge(o_var_made, 2 * i + h + 1)
                    nc.gpsimd.tensor_tensor(o_rstd[:, half], o_var[:, half], neg_half[:, half],
                                            ALU.pow).then_inc(o_rstd_made, 1)

                offset(0)
                o_rstd_of(0)
                offset(1)
                o_rstd_of(1)

            pool.wait_ge(rows_loaded, 16)
            batch(0)
            with pool.Fori(1, B - 1) as i:
                batch(i)
            batch(B - 1, last=True)

        @block.scalar
        def _(act):
            act.dma_start(x_all[:, 0, 2:4], x[0, 2 * P:T].rearrange("(t p) c -> p t c", p=P)).then_inc(x0_loaded[1], 16)
            act.dma_start(col[:], cols).then_inc(cols_loaded, 16)
            act.dma_start(row[:], rows.rearrange("(o r) c -> o r c", o=1).broadcast_to((P, 4, C))).then_inc(rows_loaded, 16)

            def weight_hi(n, raw):
                act.wait_ge(qkv_loaded[raw], 16)
                nc.scalar.copy(w["hi"][:, n], raw_qkv[:, raw]).then_inc(w_hi_made, 1)

            def abs_sum_of(n, raw, loaded):
                act.wait_ge(loaded, 16)
                if n:
                    act.wait_ge(abs_summed, n)
                nc.scalar.activation(abs_out, raw, ACT.Abs, accum_out=abs_sum[:, n:n + 1]).then_inc(abs_summed, 1)

            def xT_hi(b):
                for k in range(CK):
                    act.wait_ge(xT_summed, 2 * b + k + 1)
                    nc.scalar.copy(xT["hi"][:, k], bank[(AT_XT + k) % BANKS][:]).then_inc(xT_hi_made, 1)

            weight_hi(0, 0)
            weight_hi(1, 1)
            xT_hi(0)
            abs_sum_of(0, raw1, raw1_loaded)
            weight_hi(2, 2)
            abs_sum_of(1, raw2, raw2_loaded)
            act.wait_ge(cols_loaded, 16)

            def batch(i, first=False, last=False):
                for m in range(6):
                    act.wait_ge(l1_summed, 6 * i + m + 1)
                    if not first:
                        act.wait_ge(r_split, 8 * (i - 1) + m + 3)
                    b1 = col[:, COL_B1 + m:COL_B1 + m + 1]
                    nc.scalar.activation(g["hi"][:, m], bank[(AT_L1 + m) % BANKS][:], ACT.Gelu, bias=b1)
                    nc.scalar.activation(act32[:, m], bank[(AT_L1 + m) % BANKS][:], ACT.Gelu, bias=b1).then_inc(l1_read, 1)
                    if first and m == 3:
                        weight_hi(4, 5)
                        act.wait_ge(folded, 1)
                        nc.scalar.copy(w["hi"][:, 3].rearrange("p k c -> p (k c)"), bank[6][:]).then_inc(fold_hi_made, 1)
                for f in range(FT):
                    slot = (6 + f) % RING
                    act.wait_ge(f1_summed, 8 * i + f + 1)
                    if first and f == 0:
                        act.wait_ge(abs_summed, 2)
                    if f == 7:
                        act.wait_ge(r_split, 8 * i + 1)
                    elif f > 0:
                        act.wait_ge(g_split, 6 * i + f)
                    elif not first:
                        act.wait_ge(r_split, 8 * i)
                    b1 = col[:, COL_F1 + f:COL_F1 + f + 1]
                    nc.scalar.activation(r["hi"][:, f], bank[(AT_F1 + f) % BANKS][:], ACT.Relu, bias=b1)
                    nc.scalar.activation(act32[:, slot], bank[(AT_F1 + f) % BANKS][:], ACT.Relu, bias=b1).then_inc(f1_read, 1)
                if first:
                    act.wait_ge(fold_read, 1)
                for k in range(CK):
                    act.wait_ge(z_summed, 2 * i + k + 1)
                    nc.scalar.activation(z["hi"][:, k], bank[(AT_K + k) % BANKS][:], ACT.Identity,
                                         bias=z_bias[:, k:k + 1]).then_inc(z_hi_made, 1)
                act.wait_ge(v_read, 2 * i + 2)
                nc.scalar.copy(v["hi"][:], v32[:]).then_inc(v_hi_made, 1)

                def silu(h, ready):
                    act.wait_ge(y_read, ready)
                    nc.scalar.activation(y[:, 2 * h:2 * h + 2], y[:, 2 * h:2 * h + 2], ACT.Silu).then_inc(silu_made, 1)

                silu(0, 3 * i + 1)
                for j in range(TT):
                    act.wait_ge(s_read, 4 * i + j + 1)
                    at = slice(S_AT[j], S_AT[j] + S_COLS[j])
                    nc.scalar.copy(s["hi"][:, at], s32[:, at]).then_inc(s_hi_made, 1)
                if not last:
                    xT_hi(i + 1)
                silu(1, 3 * i + 3)

            batch(0, first=True)
            with act.Fori(1, B - 1) as i:
                batch(i)
            batch(B - 1, last=True)

        @block.vector
        def _(dve):
            STEPS = TT + 5
            HALF_STEPS = 2 + 5

            def aggregate(stats, part, mean, var, steps, ready, made, tiles=slice(0, TT)):
                even_mean, even_sq, odd_mean, odd_sq = (stats[:, tiles, n] for n in (1, 2, 4, 5))
                part, mean, var = part[:, :, tiles], mean[:, tiles], var[:, tiles]
                dve.wait_ge(steps, ready)
                nc.vector.tensor_tensor(part[:, 0], even_mean, odd_mean, ALU.add).then_inc(steps, 1)
                nc.vector.tensor_tensor(part[:, 1], even_mean, odd_mean, ALU.subtract).then_inc(steps, 1)
                nc.vector.scalar_tensor_tensor(part[:, 2], even_sq, C * EPS, odd_sq, ALU.add, ALU.add).then_inc(steps, 1)
                dve.wait_ge(steps, ready + 3)
                nc.vector.tensor_scalar(mean, part[:, 0], 0.5, None, ALU.mult).then_inc(steps, 1)
                nc.vector.scalar_tensor_tensor(part[:, 3], part[:, 1], 0.25, part[:, 1], ALU.mult, ALU.mult).then_inc(steps, 1)
                dve.wait_ge(steps, ready + 5)
                nc.vector.scalar_tensor_tensor(var, part[:, 2], 1.0 / C, part[:, 3], ALU.mult, ALU.add).then_inc(made, 1)

            def x_statistics(b, first=False):
                if not first:
                    dve.wait_ge(x_loaded, 16 * b)
                for t in range(TT):
                    if first and t % 2 == 0:
                        dve.wait_ge(x0_loaded[t // 2], 16)
                    nc.vector.bn_stats(x_stats[:, t], x_all[:, b, t]).then_inc(x_stats_made, 1)
                aggregate(x_stats, x_part, x_mean, x_var, x_stats_made, STEPS * b + TT, x_var_made)

            def x_normalise(b):
                dve.wait_ge(x_rstd_made, b + 1)
                for t in range(TT):
                    nc.vector.tensor_scalar(xn[:, t], x_all[:, b, t], x_mean[:, t:t + 1], x_rstd[:, t:t + 1],
                                            ALU.subtract, ALU.mult).then_inc(xn_made, 1)

            def xT_lo(b):
                for k in range(CK):
                    dve.wait_ge(xT_hi_made, 2 * b + k + 1)
                    nc.vector.tensor_tensor(xT["lo"][:, k], bank[(AT_XT + k) % BANKS][:],
                                            xT["hi"][:, k].bitcast(FP32), ALU.subtract).then_inc(xT_split, 1)

            x_statistics(0, first=True)
            x_normalise(0)

            def split_weight(n):
                dve.wait_ge(w_hi_made, n + 1)
                nc.vector.tensor_tensor(w["lo"][:, n], raw_qkv[:, n], w["hi"][:, n].bitcast(FP32),
                                        ALU.subtract).then_inc(w_split, 1)

            split_weight(0)
            split_weight(1)
            xT_lo(0)
            for n, raw, quant, done in ((0, raw1, w1q[:].rearrange("p a b -> p (a b)"), w1_quantized),
                                        (1, raw2, w2q[:].rearrange("p a b -> p (a b)"), w2_quantized)):
                dve.wait_ge(gamma_summed, n + 1)
                total = bank[4 + n][:, 0:1]
                nc.vector.tensor_scalar(thr[:, n:n + 1], total, 0.5 / (C * F), 0.5 * EPS,
                                        ALU.mult, ALU.add).then_inc(thr_made, 1)
                nc.vector.tensor_scalar(neg_thr[:, n:n + 1], total, -0.5 / (C * F), -0.5 * EPS,
                                        ALU.mult, ALU.add).then_inc(thr_made, 1)
                dve.wait_ge(thr_made, 2 * n + 2)
                for h in range(2):
                    part = slice(h * F, (h + 1) * F)
                    if n or h:
                        dve.wait_ge(done if h else w1_quantized, 1 if h else 2)
                    nc.vector.tensor_scalar(flags, raw[:, part], neg_thr[:, n:n + 1], None,
                                            ALU.is_lt).then_inc(flags_made, 1)
                    dve.wait_ge(flags_made, 2 * n + h + 1)
                    nc.vector.scalar_tensor_tensor(quant[:, part], raw[:, part], thr[:, n:n + 1], flags,
                                                   ALU.is_gt, ALU.subtract).then_inc(done, 1)
                if n == 0:
                    split_weight(2)
            dve.wait_ge(fold_hi_made, 1)
            nc.vector.tensor_tensor(w["lo"][:, 3].rearrange("p k c -> p (k c)"), bank[6][:],
                                    w["hi"][:, 3].rearrange("p k c -> p (k c)").bitcast(FP32),
                                    ALU.subtract).then_inc(fold_read, 1)
            dve.wait_ge(folded, 2)
            nc.vector.tensor_copy(z_bias[:], bank[7][:, 0:CK])
            nc.vector.tensor_copy(d_const[:], bank[7][:, 2 * CK:2 * CK + 1])
            nc.vector.tensor_copy(d_weight[:, :, 0], bank[7][:, CK:2 * CK]).then_inc(fold_hi_made, 1)
            dve.wait_ge(fold_hi_made, 2)
            nc.vector.tensor_tensor(d_weight[:, :, 1], bank[7][:, CK:2 * CK], d_weight[:, :, 0].bitcast(FP32),
                                    ALU.subtract).then_inc(fold_read, 1)
            dve.wait_ge(rows_loaded, 16)
            dve.wait_ge(cols_loaded, 16)
            dve.wait_ge(consts_made, 4)

            def batch(i, last=False):
                if not last:
                    x_statistics(i + 1)
                for f in range(FT):
                    dve.wait_ge(f1_read, 8 * i + f + 1)
                    nc.vector.tensor_tensor(r["lo"][:, f], act32[:, (6 + f) % RING], r["hi"][:, f].bitcast(FP32),
                                            ALU.subtract).then_inc(r_split, 1)
                if not last:
                    x_normalise(i + 1)
                for k in range(CK):
                    dve.wait_ge(z_hi_made, 2 * i + k + 1)
                    nc.vector.scalar_tensor_tensor(z["lo"][:, k], bank[(AT_K + k) % BANKS][:], z_bias[:, k:k + 1],
                                                   z["hi"][:, k].bitcast(FP32), ALU.add, ALU.subtract).then_inc(z_split, 1)
                dve.wait_ge(d_summed, i + 1)
                nc.vector.tensor_reduce(d_sum[:], bank[AT_D % BANKS][:, 0:2 * TT].rearrange("p (t e) -> p t e", e=2),
                                        mybir.AxisListType.X, ALU.add).then_inc(d_read, 1)
                dve.wait_ge(d_read, i + 1)
                nc.vector.tensor_scalar(d[:], d_sum[:], d_const[:, 0:1], None, ALU.add).then_inc(d_made, 1)

                for n in range(2):
                    dve.wait_ge(v_summed, 2 * i + n + 1)
                    nc.vector.tensor_tensor(v32[:, 2 * n:2 * n + 2],
                                            bank[(AT_V + n) % BANKS][:].rearrange("p (t c) -> p t c", t=2),
                                            row[:, ROW_B2V:ROW_B2V + 1].broadcast_to((P, 2, C)),
                                            ALU.add).then_inc(v_read, 1)

                def y_bias(at, t, tiles, ready):
                    dve.wait_ge(y_summed, ready)
                    nc.vector.tensor_tensor(y[:, t:t + tiles],
                                            bank[at % BANKS][:, 0:tiles * C].rearrange("p (t c) -> p t c", t=tiles),
                                            row[:, ROW_F2:ROW_F2 + 1].broadcast_to((P, tiles, C)),
                                            ALU.add).then_inc(y_read, 1)

                def gate(h):
                    half = slice(2 * h, 2 * h + 2)
                    dve.wait_ge(silu_made, 2 * i + h + 1)
                    nc.vector.tensor_tensor(gw[:, half], y[:, half], row[:, ROW_LNW:ROW_LNW + 1].broadcast_to((P, 2, C)),
                                            ALU.mult).then_inc(gw_made, 1)

                y_bias(AT_Y0, 0, 2, 3 * i + 1)
                dve.wait_ge(d_made, i + 1)

                def s_scale(j):
                    dve.wait_ge(s_summed, 4 * i + j + 1)
                    src = bank[(AT_S + j) % BANKS]
                    last_op = nc.vector.scalar_tensor_tensor(s32[:, S_AT[j]:S_AT[j] + P], src[:, 0:P], d[:, j:j + 1],
                                                             causal[:], ALU.add, ALU.mult)
                    if S_COLS[j] > P:
                        last_op = nc.vector.tensor_scalar(s32[:, S_AT[j] + P:S_AT[j] + S_COLS[j]], src[:, P:S_COLS[j]],
                                                          d[:, j:j + 1], INV_SCALE, ALU.add, ALU.mult)
                    last_op.then_inc(s_read, 1)

                def s_lo(j):
                    dve.wait_ge(s_hi_made, 4 * i + j + 1)
                    at = slice(S_AT[j], S_AT[j] + S_COLS[j])
                    nc.vector.tensor_tensor(s["lo"][:, at], s32[:, at], s["hi"][:, at].bitcast(FP32),
                                            ALU.subtract).then_inc(s_split, 1)

                s_scale(0)
                for j in range(1, TT):
                    s_scale(j)
                    s_lo(j - 1)
                s_lo(TT - 1)
                gate(0)
                y_bias(AT_Y1, 2, 1, 3 * i + 2)
                y_bias(AT_Y1 + 1, 3, 1, 3 * i + 3)
                if not last:
                    xT_lo(i + 1)
                gate(1)
                for h in range(2):
                    for t in (2 * h, 2 * h + 1):
                        dve.wait_ge(o_summed, 4 * i + t + 1)
                        nc.vector.bn_stats(o_stats[:, t], bank[(AT_O + t) % BANKS][:, 0:C]).then_inc(o_stats_made, 1)
                    aggregate(o_stats, o_part, o_mean, o_var, o_stats_made, HALF_STEPS * (2 * i + h) + 2, o_var_made,
                              slice(2 * h, 2 * h + 2))
                    for t in (2 * h, 2 * h + 1):
                        nc.vector.scalar_tensor_tensor(gw[:, t], bank[(AT_O + t) % BANKS][:, 0:C], o_mean[:, t:t + 1],
                                                       gw[:, t], ALU.subtract, ALU.mult).then_inc(o_read, 1)
                for h in range(2):
                    dve.wait_ge(o_rstd_made, 2 * i + h + 1)
                    dve.wait_ge(gb_made, 2 * i + h + 1)
                    dve.wait_ge(o_read, 4 * i + 2 * h + 2)
                    for t in (2 * h, 2 * h + 1):
                        last_op = nc.vector.scalar_tensor_tensor(x_all[:, i, t], gw[:, t], o_rstd[:, t:t + 1],
                                                                 x_all[:, i, t], ALU.mult, ALU.add)
                    last_op.then_inc(out_made, 1)

            batch(0)
            with dve.Fori(1, B - 1) as i:
                batch(i)
            batch(B - 1, last=True)

        @block.tensor
        def _(pe):
            def claim(i, at, first=False):
                read, per_batch, count = reading_of((at - BANKS) % FILLS)
                if at >= BANKS:
                    pe.wait_ge(read, per_batch * i + count)
                elif not first:
                    pe.wait_ge(read, per_batch * (i - 1) + count)
                elif read is xT_split:
                    pe.wait_ge(read, count - CK)
                return bank[at % BANKS]

            def transpose_x(i, b, first=False):
                for k in range(CK):
                    dst = bank[(AT_XT + k) % BANKS] if first else claim(i, AT_XT + k)
                    pe.wait_ge(xn_made, 4 * b + 4)
                    for t in range(TT):
                        last = nc.tensor.transpose(dst[:, t * P:(t + 1) * P], xn[:, t, k * P:(k + 1) * P], ident[:])
                    last.then_inc(xT_summed, 1)

            pe.wait_ge(consts_made, 4)
            for _ in range(WARM_UP):
                nc.tensor.matmul(bank[7][:, 0:P], ones[:], ident[:], start=True, stop=True)
            transpose_x(0, 0, first=True)

            def split_product(dst, pairs):
                for n, (a, b) in enumerate(pairs):
                    last = nc.tensor.matmul(dst, a, b, start=(n == 0), stop=(n == len(pairs) - 1))
                return last

            def fold_weights():
                for n in (3, 4):
                    pe.wait_ge(qkv_loaded[n], 16)
                pe.wait_ge(cols_loaded, 16)
                w2qT, w2kT = raw_qkv[:, 3], raw_qkv[:, 4]
                b2q, b2k = col[:, COL_B2:COL_B2 + CK], col[:, COL_B2 + CK:COL_B2 + 2 * CK]
                for n in range(CK):
                    last = split_product(bank[6][:, n * C:(n + 1) * C],
                                         [(w2kT[:, k, n * P:(n + 1) * P], w2qT[:, k]) for k in range(CK)])
                last.then_inc(folded, 1)
                for n in range(CK):
                    split_product(bank[7][:, n:n + 1],
                                  [(w2qT[:, k, n * P:(n + 1) * P], b2k[:, k:k + 1]) for k in range(CK)])
                    split_product(bank[7][:, CK + n:CK + n + 1],
                                  [(w2kT[:, k, n * P:(n + 1) * P], b2q[:, k:k + 1]) for k in range(CK)])
                split_product(bank[7][:, 2 * CK:2 * CK + 1],
                              [(b2q[:, k:k + 1].broadcast_to((P, P)), b2k[:, k:k + 1])
                               for k in range(CK)]).then_inc(folded, 1)

            def ffn_out(i, at, tiles):
                dst = claim(i, at)
                for n, t in enumerate(tiles):
                    last = split_product(dst[:, n * C:(n + 1) * C],
                                         [(r[part][:, f, t * P:(t + 1) * P], w2q[:, f])
                                          for part in ("lo", "hi") for f in range(FT)])
                last.then_inc(y_summed, 1)

            def batch(i, first=False, last=False):
                pe.wait_ge(xT_split, 2 * i + 2)
                for m in range(6):
                    if first:
                        pe.wait_ge(w_split, m // 2 + 1)
                    dst = claim(i, AT_L1 + m, first)
                    h = slice((m % 2) * P, (m % 2 + 1) * P)
                    split_product(dst[:], [(w[a][:, m // 2, k, h], xT[b][:, k])
                                           for a, b in FULL for k in range(CK)]).then_inc(l1_summed, 1)
                    if first and m in (1, 2):
                        pe.wait_ge(abs_summed, m)
                        nc.tensor.matmul(bank[3 + m][:, 0:1], ones[:], abs_sum[:, m - 1:m],
                                         start=True, stop=True).then_inc(gamma_summed, 1)
                    if first and m == 3:
                        fold_weights()
                        pe.wait_ge(thr_made, 4)
                if first:
                    pe.wait_ge(w1_quantized, 2)
                    pe.wait_ge(fold_read, 2)
                for f in range(FT):
                    dst = claim(i, AT_F1 + f, first)
                    split_product(dst[:], [(w1q[:, k, f * P:(f + 1) * P], xT[part][:, k])
                                           for part in ("lo", "hi") for k in range(CK)]).then_inc(f1_summed, 1)
                pe.wait_ge(g_split, 6 * i + 4)
                for n in range(CK):
                    dst = claim(i, AT_K + n)
                    h = slice(n * P, (n + 1) * P)
                    split_product(dst[:], [(w[a][:, 3, k, h], g[b][:, 2 + k])
                                           for a, b in FULL for k in range(CK)]).then_inc(z_summed, 1)
                dst = claim(i, AT_D)
                for t in range(TT):
                    done = split_product(dst[:, 2 * t:2 * t + 2],
                                         [(g[a][:, 2 + k, t * P:(t + 1) * P], d_weight[:, k])
                                          for a in ("lo", "hi") for k in range(CK)])
                done.then_inc(d_summed, 1)
                pe.wait_ge(g_split, 6 * i + 6)
                if first:
                    pe.wait_ge(w2v_split, 1)
                for n in range(2):
                    dst = claim(i, AT_V + n)
                    for t in (2 * n, 2 * n + 1):
                        done = split_product(dst[:, (t % 2) * C:(t % 2 + 1) * C],
                                             [(g[a][:, 4 + k, t * P:(t + 1) * P], w[b][:, 4, k])
                                              for a, b in FULL for k in range(CK)])
                    done.then_inc(v_summed, 1)
                pe.wait_ge(r_split, 8 * i + 8)
                if first:
                    pe.wait_ge(w2_quantized, 2)
                ffn_out(i, AT_Y0, (0, 1))
                pe.wait_ge(z_split, 2 * i + 2)
                for j in range(TT):
                    dst = claim(i, AT_S + j)
                    split_product(dst[:, 0:S_COLS[j]], [(z[a][:, k, j * P:(j + 1) * P], g[b][:, k, j * P:T])
                                                        for a, b in FULL for k in range(CK)]).then_inc(s_summed, 1)
                ffn_out(i, AT_Y1, (2,))
                ffn_out(i, AT_Y1 + 1, (3,))
                if not last:
                    transpose_x(i, i + 1)
                pe.wait_ge(v_split, i + 1)
                for t in range(TT):
                    pe.wait_ge(s_split, 4 * i + t + 1)
                    dst = claim(i, AT_O + t)
                    split_product(dst[:, 0:C], [(s[a][:, S_AT[j] + (t - j) * P:S_AT[j] + (t - j + 1) * P], v[b][:, j])
                                                for a, b in FULL for j in range(t + 1)]).then_inc(o_summed, 1)

            batch(0, first=True)
            with pe.Fori(1, B - 1) as i:
                batch(i)
            batch(B - 1, last=True)


def kernel(**inputs):
    import numpy as np
    import concourse.bacc as bacc
    from concourse.bass_utils import run_bass_kernel_spmd

    def by_partition(name):
        return np.asarray(inputs[name]).reshape(-1, P).T

    arrays = {"x": np.ascontiguousarray(inputs["L0_attn_x"])}
    for name in ("W1q", "W1k", "W1v", "W2v"):
        arrays[name] = np.ascontiguousarray(inputs["L0_attn_" + name])
    for name in ("W2q", "W2k"):
        arrays[name] = np.ascontiguousarray(np.asarray(inputs["L0_attn_" + name]).T)
    arrays["w1t"] = np.ascontiguousarray(np.asarray(inputs["L0_ffn_W1"]).T)
    arrays["w2t"] = np.ascontiguousarray(np.asarray(inputs["L0_ffn_W2"]).T)
    arrays["cols"] = np.ascontiguousarray(np.concatenate(
        [by_partition(n) for n in ("L0_attn_b1q", "L0_attn_b1k", "L0_attn_b1v", "L0_attn_b2q", "L0_attn_b2k",
                                   "L0_ffn_b1")], axis=1))
    arrays["rows"] = np.ascontiguousarray(np.stack(
        [np.asarray(inputs[n]) for n in ("L0_attn_b2v", "L0_ffn_b2", "L0_attn_ln_w", "L0_attn_ln_b")]))

    nc = bacc.Bacc("TRN2", target_bir_lowering=False, num_devices=1, dynamic_dma_scratch_size=1024)
    aps = {n: nc.dram_tensor(f"in_{n}", a.shape, FP32, kind="ExternalInput").ap() for n, a in arrays.items()}
    out = nc.dram_tensor("out", (B, T, C), FP32, kind="ExternalOutput").ap()
    gated_block(nc, aps["x"], [aps[n] for n in ("W1q", "W1k", "W1v", "W2q", "W2k", "W2v")],
                aps["w1t"], aps["w2t"], aps["cols"], aps["rows"], out)
    result = run_bass_kernel_spmd(nc, [{f"in_{n}": a for n, a in arrays.items()}], core_ids=[0])
    return result.results[0]["out"]
```

```python
import concourse.bass as bass
from concourse import mybir
from contextlib import ExitStack

FP32 = mybir.dt.float32
FP32R = mybir.dt.float32r
ALU = mybir.AluOpType
ACT = mybir.ActivationFunctionType

P = 128
B, T, C = 8, 512, 256
F = 4 * C
TT = T // P
CK = C // P
FT = F // P
EPS = 1e-5
INV_SCALE = 1.0 / float((C * T) ** 0.5)

FULL = (("hi", "hi"), ("lo", "hi"), ("hi", "lo"))

AT_L1, AT_F1, AT_K, AT_V, AT_D, AT_Y0, AT_S, AT_Y1, AT_O = 0, 6, 14, 16, 18, 19, 20, 24, 28
FILLS, BANKS = 32, 8
AT_NONE = (26, 27)
AT_X0 = 2
S_COLS = [T - j * P for j in range(TT)]
S_AT = [sum(S_COLS[:j]) for j in range(TT)]
COL_B1, COL_B2, COL_F1 = 0, 6, 10
ROW_B2V, ROW_F2, ROW_LNW, ROW_LNB = range(4)
WARM_UP = 9
RING = 7


def gated_block(nc, x, x_t, x_norm_rows, w_qkv, w1t, w2t, cols, rows, out):
    ctx = ExitStack()
    with ctx:
        def sb(name, shape, dt=FP32):
            return ctx.enter_context(nc.sbuf_tensor(name, shape, dt))

        def sem(name):
            return ctx.enter_context(nc.semaphore(name))

        ident = sb("ident", [P, P])
        ones = sb("ones", [P, P])
        ones_r = sb("ones_r", [P, P], FP32R)
        causal = sb("causal", [P, P])
        neg_half = sb("neg_half", [P, TT])
        col = sb("col", [P, 18])
        row = sb("row", [P, 4, C])
        w = {"hi": sb("w_hi", [P, 5, CK, C], FP32R), "lo": sb("w_lo", [P, 5, CK, C], FP32R)}
        z_bias = sb("z_bias", [P, CK])
        d_weight = sb("d_weight", [P, CK])
        d_const = sb("d_const", [P, 1])
        w1q = sb("w1q", [P, CK, F], FP32R)
        w2q = sb("w2q", [P, FT, C], FP32R)
        abs_sum = sb("abs_sum", [P, 2])
        thr = sb("thr", [P, 2])
        neg_thr = sb("neg_thr", [P, 2])
        x_all = sb("x_all", [P, B, TT, C])
        xn = sb("xn", [P, TT, C])
        y = sb("y", [P, TT, C])
        gw = sb("gw", [P, TT, C])
        v32 = sb("v32", [P, TT, C])
        v = {"hi": sb("v_hi", [P, TT, C], FP32R), "lo": sb("v_lo", [P, TT, C], FP32R)}
        x_stats = sb("x_stats", [P, TT, 6])
        x_part = sb("x_part", [P, 4, TT])
        x_norm = sb("x_norm", [P, 2, TT])
        x_mean, x_rstd = x_norm[:, 0], x_norm[:, 1]
        x_var = sb("x_var", [P, TT])
        o_stats = sb("o_stats", [P, TT, 6])
        o_part = sb("o_part", [P, 4, TT])
        o_mean = sb("o_mean", [P, TT])
        o_var = sb("o_var", [P, TT])
        o_rstd = sb("o_rstd", [P, TT])
        xT32 = y[:].rearrange("p t c -> p (t c)").rearrange("p (k t) -> p k t", k=CK)
        x_norm_all = xn[:].rearrange("p t c -> p (t c)")
        x_mean_all, x_rstd_all = (x_norm_all.rearrange("q (p n t) -> q n t p", n=2, t=TT)[:, n] for n in range(2))
        xT = {"hi": sb("xT_hi", [P, CK, T], FP32R), "lo": sb("xT_lo", [P, CK, T], FP32R)}
        act32 = sb("act32", [P, RING, T])
        g = {"hi": sb("g_hi", [P, 6, T], FP32R), "lo": sb("g_lo", [P, 6, T], FP32R)}
        r = {"hi": sb("r_hi", [P, FT, T], FP32R), "lo": sb("r_lo", [P, FT, T], FP32R)}
        z = {"hi": sb("z_hi", [P, CK, T], FP32R), "lo": sb("z_lo", [P, CK, T], FP32R)}
        e32 = sb("e32", [P, T])
        e = {"hi": sb("e_hi", [P, T], FP32R), "lo": sb("e_lo", [P, T], FP32R)}
        d = sb("d", [P, TT])
        s32 = sb("s32", [P, sum(S_COLS)])
        s = {"hi": sb("s_hi", [P, sum(S_COLS)], FP32R), "lo": sb("s_lo", [P, sum(S_COLS)], FP32R)}
        bank = [ctx.enter_context(nc.psum_tensor(f"bank{n}", [P, T], FP32)) for n in range(BANKS)]
        GAMMA = (bank[4][:, 0:1], bank[5][:, 0:1])
        FOLD_Z, FOLD_DW, FOLD_D = bank[7][:, 0:CK], bank[7][:, CK:2 * CK], bank[7][:, 2 * CK:2 * CK + 1]
        RAW1, RAW2 = B - 4, B - 2
        raw1 = x_all[:, RAW1:RAW1 + 2].rearrange("p a t c -> p (a t c)")
        raw2 = x_all[:, RAW2:RAW2 + 2].rearrange("p a t c -> p (a t c)")
        raw_qkv = act32[:, 0:6].rearrange("p n (k c) -> p n k c", k=CK)
        flags = s32[:, 0:F]
        abs_out = r["lo"][:, 0:4].rearrange("p a t -> p (a t)")

        x0_loaded = [sem(f"x0_loaded{h}") for h in range(2)]
        x_loaded, cols_loaded, rows_loaded = sem("x_loaded"), sem("cols_loaded"), sem("rows_loaded")
        qkv_loaded = [sem(f"qkv_loaded{n}") for n in range(6)]
        raw1_loaded, raw2_loaded = sem("raw1_loaded"), sem("raw2_loaded")
        ident_zero, consts_made, causal_filled = sem("ident_zero"), sem("consts_made"), sem("causal_filled")
        ones_rounded = sem("ones_rounded")
        w_hi_made, w_split, w2v_hi_made, w2v_split = (
            sem("w_hi_made"), sem("w_split"), sem("w2v_hi_made"), sem("w2v_split"))
        folded, fold_hi_made, fold_read = sem("folded"), sem("fold_hi_made"), sem("fold_read")
        abs_summed, gamma_summed, thr_made = sem("abs_summed"), sem("gamma_summed"), sem("thr_made")
        flags_made, w1_quantized, w2_quantized = sem("flags_made"), sem("w1_quantized"), sem("w2_quantized")
        x_stats_made, x_var_made, x_rstd_made, xn_made = (
            sem("x_stats_made"), sem("x_var_made"), sem("x_rstd_made"), sem("xn_made"))
        xT_summed, l1_summed, f1_summed, z_summed, d_summed, v_summed, y_summed, s_summed, o_summed = (
            sem(n) for n in ("xT_summed", "l1_summed", "f1_summed", "z_summed", "d_summed", "v_summed", "y_summed",
                             "s_summed", "o_summed"))
        l1_read, f1_read, d_read, v_read, y_read, s_read, o_read = (
            sem(n) for n in ("l1_read", "f1_read", "d_read", "v_read", "y_read", "s_read", "o_read"))
        xT_loaded, x_norm_stored, x_norm_loaded = sem("xT_loaded"), sem("x_norm_stored"), sem("x_norm_loaded")
        xT_centred, xT_normalised = sem("xT_centred"), sem("xT_normalised")
        xT_hi_made, xT_split = sem("xT_hi_made"), sem("xT_split")
        g_split, r_split = sem("g_split"), sem("r_split")
        e_half, e_made, e_hi_made, e_split = sem("e_half"), sem("e_made"), sem("e_hi_made"), sem("e_split")
        z_hi_made, z_split = sem("z_hi_made"), sem("z_split")
        v_hi_made, v_split = sem("v_hi_made"), sem("v_split")
        s_hi_made, s_split = sem("s_hi_made"), sem("s_split")
        silu_made, gw_made, last_gw_made, gb_part, gb_made = (
            sem("silu_made"), sem("gw_made"), sem("last_gw_made"), sem("gb_part"), sem("gb_made"))
        o_stats_made, o_var_made, o_rstd_made = sem("o_stats_made"), sem("o_var_made"), sem("o_rstd_made")
        out_made, stored = sem("out_made"), sem("stored")

        STAGES = ((AT_L1, 6, l1_read, 6, 0), (AT_F1, FT, f1_read, FT, 0), (AT_K, 2, z_split, 2, 0),
                  (AT_V, 2, v_read, 2, 0), (AT_D, 1, d_read, TT, TT - 1), (AT_Y0, 1, y_read, 3, 0),
                  (AT_S, TT, s_read, TT, 0), (AT_Y1, 2, y_read, 3, 1),
                  (AT_O, TT, o_read, TT, 0))

        def reading_of(at):
            if at in AT_NONE:
                at -= BANKS
            for first, fills, read, per_batch, before in STAGES:
                if first <= at < first + fills:
                    return read, per_batch, before + at - first + 1

        block = ctx.enter_context(nc.Block())

        @block.sync
        def _(sp):
            def load_x(b):
                sp.dma_start(x_all[:, b], x[b].rearrange("(t p) c -> p t c", p=P)).then_inc(x_loaded, 16)

            def load_square(n):
                sp.dma_start(raw_qkv[:, n], w_qkv[n].rearrange("(k p) c -> p k c", p=P)).then_inc(qkv_loaded[n], 16)

            sp.dma_start(x_all[:, 0, 0:2], x[0, 0:2 * P].rearrange("(t p) c -> p t c", p=P)).then_inc(x0_loaded[0], 16)
            load_square(3)
            load_square(4)
            load_square(0)
            load_square(1)
            sp.dma_start(raw1.rearrange("p (k f) -> p k f", k=CK),
                         w1t.rearrange("(k p) f -> p k f", p=P)).then_inc(raw1_loaded, 16)
            load_square(2)
            sp.dma_start(raw2.rearrange("p (f c) -> p f c", f=FT),
                         w2t.rearrange("(f p) c -> p f c", p=P)).then_inc(raw2_loaded, 16)
            load_square(5)
            for b in range(1, RAW1):
                if b > 1:
                    sp.wait_ge(x_loaded, 16 * b - 16)
                load_x(b)

            def load_xT(b):
                sp.dma_start(xT32, x_t[b].rearrange("(k p) t -> p k t", p=P)).then_inc(xT_loaded, 16)

            def spread_x_norm(b):
                sp.wait_ge(x_rstd_made, b + 1)
                sp.dma_start(x_norm_rows[b], x_norm[:]).then_inc(x_norm_stored, 16)
                sp.wait_ge(x_norm_stored, 16 * b)
                sp.dma_start(x_norm_all, x_norm_rows[b].rearrange("(o p) n t -> o (p n t)", o=1).broadcast_to((P, 2 * T))
                             ).then_inc(x_norm_loaded, 16)

            load_xT(1)
            sp.wait_ge(xT_summed, CK)
            spread_x_norm(1)
            sp.wait_ge(w1_quantized, 2)
            sp.wait_ge(w2_quantized, 2)
            with sp.Fori(RAW1, B) as b:
                sp.wait_ge(x_loaded, 16 * b - 16)
                load_x(b)

            def store(b, t, tiles, ready):
                sp.wait_ge(out_made, ready)
                sp.dma_start(out[b, t * P:(t + tiles) * P].rearrange("(t p) c -> p t c", p=P),
                             x_all[:, b, t:t + tiles]).then_inc(stored, 16)

            with sp.Fori(1, B - 1) as i:
                sp.wait_ge(gb_made, 2 * i)
                load_xT(i + 1)
                store(i - 1, 0, 2, 2 * i - 1)
                store(i - 1, 2, 2, 2 * i)
                spread_x_norm(i + 1)
            store(B - 2, 0, 2, 2 * B - 3)
            store(B - 2, 2, 2, 2 * B - 2)
            store(B - 1, 0, 2, 2 * B - 1)
            store(B - 1, 2, 1, 2 * B)
            store(B - 1, 3, 1, 2 * B + 1)
            sp.wait_ge(stored, 16 * (2 * B + 1))

        @block.gpsimd
        def _(pool):
            nc.gpsimd.memset(ident[:], 0.0).then_inc(ident_zero, 1)
            nc.gpsimd.memset(neg_half[:], -0.5).then_inc(consts_made, 1)
            pool.wait_ge(ident_zero, 1)
            nc.gpsimd.affine_select(out=ident[:], in_=ident[:], compare_op=ALU.not_equal, fill=1.0, base=0,
                                    pattern=[[-1, P]], channel_multiplier=1).then_inc(consts_made, 1)
            nc.gpsimd.memset(ones[:], 1.0).then_inc(consts_made, 1)
            nc.gpsimd.memset(causal[:], INV_SCALE).then_inc(causal_filled, 1)
            pool.wait_ge(causal_filled, 1)
            nc.gpsimd.affine_select(out=causal[:], in_=causal[:], compare_op=ALU.is_ge, fill=0.0, base=0,
                                    pattern=[[1, P]], channel_multiplier=-1).then_inc(consts_made, 1)

            def x_rstd_of(b):
                pool.wait_ge(x_var_made, b + 1)
                nc.gpsimd.tensor_tensor(x_rstd, x_var[:], neg_half[:], ALU.pow).then_inc(x_rstd_made, 1)

            pool.wait_ge(consts_made, 4)
            x_rstd_of(0)
            pool.wait_ge(qkv_loaded[5], 16)
            nc.gpsimd.tensor_copy(w["hi"][:, 4], raw_qkv[:, 5]).then_inc(w2v_hi_made, 1)
            pool.wait_ge(w2v_hi_made, 1)
            nc.gpsimd.tensor_tensor(w["lo"][:, 4], raw_qkv[:, 5], w["hi"][:, 4].bitcast(FP32),
                                    ALU.subtract).then_inc(w2v_split, 1)

            def xT_normalise(b):
                pool.wait_ge(xT_loaded, 16 * b)
                pool.wait_ge(x_norm_loaded, 16 * b)
                for k in range(CK):
                    half = xT32[:, k].rearrange("q (t p) -> q t p", t=TT)
                    nc.gpsimd.tensor_tensor(half, half, x_mean_all, ALU.subtract).then_inc(xT_centred, 1)
                    pool.wait_ge(xT_centred, CK * (b - 1) + k + 1)
                    nc.gpsimd.tensor_tensor(half, half, x_rstd_all, ALU.mult).then_inc(xT_normalised, 1)

            def batch(i, first=False, last=False):
                for m in range(6):
                    pool.wait_ge(l1_read, 6 * i + m + 1)
                    nc.gpsimd.tensor_tensor(g["lo"][:, m], act32[:, m], g["hi"][:, m].bitcast(FP32),
                                            ALU.subtract).then_inc(g_split, 1)
                    if not last and m == (2 if first else 1):
                        x_rstd_of(i + 1)
                if not last:
                    xT_normalise(i + 1)
                pool.wait_ge(v_hi_made, i + 1)
                nc.gpsimd.tensor_tensor(v["lo"][:], v32[:], v["hi"][:].bitcast(FP32),
                                        ALU.subtract).then_inc(v_split, 1)

                def offset(t, tiles, n, gate):
                    part = slice(t, t + tiles)
                    pool.wait_ge(*gate)
                    nc.gpsimd.tensor_tensor(y[:, part], y[:, part], row[:, ROW_LNB:ROW_LNB + 1].broadcast_to((P, tiles, C)),
                                            ALU.mult).then_inc(gb_part, 1)
                    pool.wait_ge(gb_part, 2 * i + n)
                    nc.gpsimd.tensor_tensor(x_all[:, i, part], x_all[:, i, part], y[:, part],
                                            ALU.add).then_inc(gb_made, 1)

                def o_rstd_of(h):
                    half = slice(2 * h, 2 * h + 2)
                    pool.wait_ge(o_var_made, 2 * i + h + 1)
                    nc.gpsimd.tensor_tensor(o_rstd[:, half], o_var[:, half], neg_half[:, half],
                                            ALU.pow).then_inc(o_rstd_made, 1)

                if last:
                    pool.wait_ge(silu_made, 2 * i + 1)
                    nc.gpsimd.tensor_tensor(gw[:, 0:2], y[:, 0:2], row[:, ROW_LNW:ROW_LNW + 1].broadcast_to((P, 2, C)),
                                            ALU.mult).then_inc(last_gw_made, 1)
                    offset(0, 2, 1, (last_gw_made, 1))
                    offset(2, 1, 2, (gw_made, 2 * i + 1))
                    o_rstd_of(0)
                    offset(3, 1, 3, (gw_made, 2 * i + 2))
                else:
                    offset(0, 2, 1, (gw_made, 2 * i + 1))
                    offset(2, 2, 2, (gw_made, 2 * i + 2))
                    o_rstd_of(0)
                o_rstd_of(1)

            pool.wait_ge(rows_loaded, 16)
            batch(0, first=True)
            with pool.Fori(1, B - 1) as i:
                batch(i)
            batch(B - 1, last=True)

        @block.scalar
        def _(act):
            act.dma_start(x_all[:, 0, 2:4], x[0, 2 * P:T].rearrange("(t p) c -> p t c", p=P)).then_inc(x0_loaded[1], 16)
            act.dma_start(col[:], cols).then_inc(cols_loaded, 16)

            def weight_hi(n, raw):
                act.wait_ge(qkv_loaded[raw], 16)
                nc.scalar.copy(w["hi"][:, n], raw_qkv[:, raw]).then_inc(w_hi_made, 1)

            def abs_sum_of(n, raw, loaded):
                act.wait_ge(loaded, 16)
                if n:
                    act.wait_ge(abs_summed, n)
                nc.scalar.activation(abs_out, raw, ACT.Abs, accum_out=abs_sum[:, n:n + 1]).then_inc(abs_summed, 1)

            def xT_hi(b):
                act.wait_ge(f1_summed, 8 * b)
                for k in range(CK):
                    act.wait_ge(xT_normalised, CK * (b - 1) + k + 1)
                    nc.scalar.copy(xT["hi"][:, k], xT32[:, k]).then_inc(xT_hi_made, 1)

            weight_hi(0, 0)
            weight_hi(1, 1)
            act.dma_start(row[:], rows.rearrange("(o r) c -> o r c", o=1).broadcast_to((P, 4, C))).then_inc(rows_loaded, 16)
            for k in range(CK):
                act.wait_ge(xT_summed, k + 1)
                nc.scalar.copy(xT["hi"][:, k], bank[AT_X0 + k][:]).then_inc(xT_hi_made, 1)
            act.wait_ge(folded, 1)
            nc.scalar.copy(w["hi"][:, 3].rearrange("p k c -> p (k c)"), bank[6][:]).then_inc(fold_hi_made, 1)
            abs_sum_of(0, raw1, raw1_loaded)
            weight_hi(2, 2)
            act.wait_ge(cols_loaded, 16)

            def batch(i, first=False, last=False):
                for m in range(6):
                    act.wait_ge(l1_summed, 6 * i + m + 1)
                    if not first:
                        act.wait_ge(r_split, 8 * (i - 1) + m + 3)
                    elif m < 3:
                        act.wait_ge(w_split, m + 1)
                    else:
                        act.wait_ge(*((folded, 2) if m < 5 else (w2v_split, 1)))
                    b1 = col[:, COL_B1 + m:COL_B1 + m + 1]
                    nc.scalar.activation(g["hi"][:, m], bank[(AT_L1 + m) % BANKS][:], ACT.Gelu, bias=b1)
                    nc.scalar.activation(act32[:, m], bank[(AT_L1 + m) % BANKS][:], ACT.Gelu, bias=b1).then_inc(l1_read, 1)
                    if first and m == 2:
                        abs_sum_of(1, raw2, raw2_loaded)
                for f in range(FT):
                    slot = (6 + f) % RING
                    act.wait_ge(f1_summed, 8 * i + f + 1)
                    if first and f == 0:
                        act.wait_ge(abs_summed, 2)
                    if f == 7:
                        act.wait_ge(r_split, 8 * i + 1)
                    elif f > 0:
                        act.wait_ge(g_split, 6 * i + f)
                        if slot == 2:
                            act.wait_ge(e_half, i + 1)
                        elif slot == 3:
                            act.wait_ge(e_made, i + 1)
                    elif not first:
                        act.wait_ge(r_split, 8 * i)
                    b1 = col[:, COL_F1 + f:COL_F1 + f + 1]
                    nc.scalar.activation(r["hi"][:, f], bank[(AT_F1 + f) % BANKS][:], ACT.Relu, bias=b1)
                    nc.scalar.activation(act32[:, slot], bank[(AT_F1 + f) % BANKS][:], ACT.Relu, bias=b1).then_inc(f1_read, 1)
                if first:
                    act.wait_ge(fold_read, 1)
                for k in range(CK):
                    act.wait_ge(z_summed, 2 * i + k + 1)
                    nc.scalar.activation(z["hi"][:, k], bank[(AT_K + k) % BANKS][:], ACT.Identity,
                                         bias=z_bias[:, k:k + 1]).then_inc(z_hi_made, 1)
                if not last:
                    xT_hi(i + 1)
                act.wait_ge(v_read, 2 * i + 2)
                nc.scalar.copy(v["hi"][:], v32[:]).then_inc(v_hi_made, 1)

                def silu(t, tiles, ready):
                    act.wait_ge(y_read, ready)
                    nc.scalar.activation(y[:, t:t + tiles], y[:, t:t + tiles], ACT.Silu).then_inc(silu_made, 1)

                silu(0, 2, 3 * i + 1)
                for j in range(TT):
                    act.wait_ge(s_read, 4 * i + j + 1)
                    at = slice(S_AT[j], S_AT[j] + S_COLS[j])
                    nc.scalar.copy(s["hi"][:, at], s32[:, at]).then_inc(s_hi_made, 1)
                if not last:
                    silu(2, 2, 3 * i + 3)
                else:
                    silu(2, 1, 3 * i + 2)
                    silu(3, 1, 3 * i + 3)

            batch(0, first=True)
            with act.Fori(1, B - 1) as i:
                batch(i)
            batch(B - 1, last=True)

        @block.vector
        def _(dve):
            STEPS = TT + 5
            HALF_STEPS = 2 + 5

            def aggregate(stats, part, mean, var, steps, ready, made, tiles=slice(0, TT)):
                even_mean, even_sq, odd_mean, odd_sq = (stats[:, tiles, n] for n in (1, 2, 4, 5))
                part, mean, var = part[:, :, tiles], mean[:, tiles], var[:, tiles]
                dve.wait_ge(steps, ready)
                nc.vector.tensor_tensor(part[:, 0], even_mean, odd_mean, ALU.add).then_inc(steps, 1)
                nc.vector.tensor_tensor(part[:, 1], even_mean, odd_mean, ALU.subtract).then_inc(steps, 1)
                nc.vector.scalar_tensor_tensor(part[:, 2], even_sq, C * EPS, odd_sq, ALU.add, ALU.add).then_inc(steps, 1)
                dve.wait_ge(steps, ready + 3)
                nc.vector.tensor_scalar(mean, part[:, 0], 0.5, None, ALU.mult).then_inc(steps, 1)
                nc.vector.scalar_tensor_tensor(part[:, 3], part[:, 1], 0.25, part[:, 1], ALU.mult, ALU.mult).then_inc(steps, 1)
                dve.wait_ge(steps, ready + 5)
                nc.vector.scalar_tensor_tensor(var, part[:, 2], 1.0 / C, part[:, 3], ALU.mult, ALU.add).then_inc(made, 1)

            def x_statistics(b, first=False, second=False):
                if not first:
                    dve.wait_ge(x_loaded, 16 * b)
                    if not second:
                        dve.wait_ge(x_norm_stored, 16 * b - 16)
                for t in range(TT):
                    if first and t % 2 == 0:
                        dve.wait_ge(x0_loaded[t // 2], 16)
                    nc.vector.bn_stats(x_stats[:, t], x_all[:, b, t]).then_inc(x_stats_made, 1)
                aggregate(x_stats, x_part, x_mean, x_var, x_stats_made, STEPS * b + TT, x_var_made)

            def x_normalise0():
                dve.wait_ge(x_rstd_made, 1)
                for t in range(TT):
                    nc.vector.tensor_scalar(xn[:, t], x_all[:, 0, t], x_mean[:, t:t + 1], x_rstd[:, t:t + 1],
                                            ALU.subtract, ALU.mult).then_inc(xn_made, 1)

            def xT_lo(b, src):
                for k in range(CK):
                    dve.wait_ge(xT_hi_made, 2 * b + k + 1)
                    nc.vector.tensor_tensor(xT["lo"][:, k], src[k], xT["hi"][:, k].bitcast(FP32),
                                            ALU.subtract).then_inc(xT_split, 1)

            x_statistics(0, first=True)
            x_normalise0()

            def split_weight(n):
                dve.wait_ge(w_hi_made, n + 1)
                nc.vector.tensor_tensor(w["lo"][:, n], raw_qkv[:, n], w["hi"][:, n].bitcast(FP32),
                                        ALU.subtract).then_inc(w_split, 1)

            split_weight(0)
            split_weight(1)
            xT_lo(0, [bank[AT_X0 + k][:] for k in range(CK)])
            dve.wait_ge(consts_made, 4)
            nc.vector.tensor_copy(ones_r[:], ones[:]).then_inc(ones_rounded, 1)

            def thresholds(n, total):
                dve.wait_ge(gamma_summed, n + 1)
                nc.vector.tensor_scalar(thr[:, n:n + 1], total, 0.5 / (C * F), 0.5 * EPS,
                                        ALU.mult, ALU.add).then_inc(thr_made, 1)
                nc.vector.tensor_scalar(neg_thr[:, n:n + 1], total, -0.5 / (C * F), -0.5 * EPS,
                                        ALU.mult, ALU.add).then_inc(thr_made, 1)

            def quantise(n, raw, quant, done):
                dve.wait_ge(thr_made, 2 * n + 2)
                for h in range(2):
                    part = slice(h * F, (h + 1) * F)
                    if n or h:
                        dve.wait_ge(done if h else w1_quantized, 1 if h else 2)
                    nc.vector.tensor_scalar(flags, raw[:, part], neg_thr[:, n:n + 1], None,
                                            ALU.is_lt).then_inc(flags_made, 1)
                    dve.wait_ge(flags_made, 2 * n + h + 1)
                    nc.vector.scalar_tensor_tensor(quant[:, part], raw[:, part], thr[:, n:n + 1], flags,
                                                   ALU.is_gt, ALU.subtract).then_inc(done, 1)

            dve.wait_ge(fold_hi_made, 1)
            nc.vector.tensor_tensor(w["lo"][:, 3].rearrange("p k c -> p (k c)"), bank[6][:],
                                    w["hi"][:, 3].rearrange("p k c -> p (k c)").bitcast(FP32),
                                    ALU.subtract).then_inc(fold_read, 1)
            split_weight(2)
            thresholds(0, GAMMA[0])
            quantise(0, raw1, w1q[:].rearrange("p a b -> p (a b)"), w1_quantized)
            dve.wait_ge(folded, 2)
            nc.vector.tensor_copy(z_bias[:], FOLD_Z)
            nc.vector.tensor_copy(d_const[:], FOLD_D)
            nc.vector.tensor_copy(d_weight[:], FOLD_DW).then_inc(fold_read, 1)
            dve.wait_ge(rows_loaded, 16)
            dve.wait_ge(cols_loaded, 16)

            def batch(i, first=False, last=False):
                if not last:
                    x_statistics(i + 1, second=first)
                dve.wait_ge(l1_read, 6 * i + 3)
                nc.vector.tensor_scalar(e32[:], act32[:, 2], d_weight[:, 0:1], None, ALU.mult).then_inc(e_half, 1)
                dve.wait_ge(l1_read, 6 * i + 4)
                dve.wait_ge(e_half, i + 1)
                nc.vector.scalar_tensor_tensor(e32[:], act32[:, 3], d_weight[:, 1:2], e32[:],
                                               ALU.mult, ALU.add).then_inc(e_made, 1)
                dve.wait_ge(e_made, i + 1)
                nc.vector.tensor_copy(e["hi"][:], e32[:]).then_inc(e_hi_made, 1)
                dve.wait_ge(e_hi_made, i + 1)
                nc.vector.tensor_tensor(e["lo"][:], e32[:], e["hi"][:].bitcast(FP32), ALU.subtract).then_inc(e_split, 1)
                if first:
                    thresholds(1, GAMMA[1])
                    quantise(1, raw2, w2q[:].rearrange("p a b -> p (a b)"), w2_quantized)
                for f in range(FT):
                    dve.wait_ge(f1_read, 8 * i + f + 1)
                    nc.vector.tensor_tensor(r["lo"][:, f], act32[:, (6 + f) % RING], r["hi"][:, f].bitcast(FP32),
                                            ALU.subtract).then_inc(r_split, 1)
                for k in range(CK):
                    dve.wait_ge(z_hi_made, 2 * i + k + 1)
                    nc.vector.scalar_tensor_tensor(z["lo"][:, k], bank[(AT_K + k) % BANKS][:], z_bias[:, k:k + 1],
                                                   z["hi"][:, k].bitcast(FP32), ALU.add, ALU.subtract).then_inc(z_split, 1)
                for n in range(2):
                    dve.wait_ge(v_summed, 2 * i + n + 1)
                    nc.vector.tensor_tensor(v32[:, 2 * n:2 * n + 2],
                                            bank[(AT_V + n) % BANKS][:].rearrange("p (t c) -> p t c", t=2),
                                            row[:, ROW_B2V:ROW_B2V + 1].broadcast_to((P, 2, C)),
                                            ALU.add).then_inc(v_read, 1)

                def y_bias(at, t, tiles, ready):
                    dve.wait_ge(y_summed, ready)
                    nc.vector.tensor_tensor(y[:, t:t + tiles],
                                            bank[at % BANKS][:, 0:tiles * C].rearrange("p (t c) -> p t c", t=tiles),
                                            row[:, ROW_F2:ROW_F2 + 1].broadcast_to((P, tiles, C)),
                                            ALU.add).then_inc(y_read, 1)

                def gate(t, tiles, n):
                    part = slice(t, t + tiles)
                    dve.wait_ge(silu_made, 2 * i + n)
                    nc.vector.tensor_tensor(gw[:, part], y[:, part], row[:, ROW_LNW:ROW_LNW + 1].broadcast_to((P, tiles, C)),
                                            ALU.mult).then_inc(gw_made, 1)

                if not last:
                    xT_lo(i + 1, [xT32[:, k] for k in range(CK)])
                dve.wait_ge(d_summed, i + 1)
                for t in range(TT):
                    at = slice(t * P, (t + 1) * P)
                    nc.vector.scalar_tensor_tensor(e32[:, at], bank[AT_D % BANKS][:, at], d_const[:, 0:1],
                                                   ident[:], ALU.add, ALU.mult, accum_out=d[:, t:t + 1]).then_inc(d_read, 1)
                if not last:
                    dve.wait_ge(xT_split, 2 * i + 4)
                y_bias(AT_Y0, 0, 2, 3 * i + 1)
                dve.wait_ge(d_read, 4 * i + 4)

                def s_scale(j):
                    dve.wait_ge(s_summed, 4 * i + j + 1)
                    src = bank[(AT_S + j) % BANKS]
                    last_op = nc.vector.scalar_tensor_tensor(s32[:, S_AT[j]:S_AT[j] + P], src[:, 0:P], d[:, j:j + 1],
                                                             causal[:], ALU.add, ALU.mult)
                    if S_COLS[j] > P:
                        last_op = nc.vector.tensor_scalar(s32[:, S_AT[j] + P:S_AT[j] + S_COLS[j]], src[:, P:S_COLS[j]],
                                                          d[:, j:j + 1], INV_SCALE, ALU.add, ALU.mult)
                    last_op.then_inc(s_read, 1)

                def s_lo(j):
                    dve.wait_ge(s_hi_made, 4 * i + j + 1)
                    at = slice(S_AT[j], S_AT[j] + S_COLS[j])
                    nc.vector.tensor_tensor(s["lo"][:, at], s32[:, at], s["hi"][:, at].bitcast(FP32),
                                            ALU.subtract).then_inc(s_split, 1)

                s_scale(0)
                for j in range(1, TT):
                    s_scale(j)
                    s_lo(j - 1)
                s_lo(TT - 1)
                if not last:
                    gate(0, 2, 1)
                y_bias(AT_Y1, 2, 1, 3 * i + 2)

                def bn_stats(t):
                    dve.wait_ge(o_summed, 4 * i + t + 1)
                    nc.vector.bn_stats(o_stats[:, t], bank[(AT_O + t) % BANKS][:, 0:C]).then_inc(o_stats_made, 1)

                def centre(tiles):
                    for t in tiles:
                        nc.vector.scalar_tensor_tensor(gw[:, t], bank[(AT_O + t) % BANKS][:, 0:C], o_mean[:, t:t + 1],
                                                       gw[:, t], ALU.subtract, ALU.mult).then_inc(o_read, 1)

                def finish(tiles, rstd, offset):
                    dve.wait_ge(o_rstd_made, 2 * i + rstd)
                    dve.wait_ge(gb_made, 2 * i + offset)
                    dve.wait_ge(o_read, 4 * i + tiles[-1] + 1)
                    for t in tiles:
                        last_op = nc.vector.scalar_tensor_tensor(x_all[:, i, t], gw[:, t], o_rstd[:, t:t + 1],
                                                                 x_all[:, i, t], ALU.mult, ALU.add)
                    last_op.then_inc(out_made, 1)

                def statistics(h):
                    for t in (2 * h, 2 * h + 1):
                        bn_stats(t)
                    aggregate(o_stats, o_part, o_mean, o_var, o_stats_made, HALF_STEPS * (2 * i + h) + 2,
                              o_var_made, slice(2 * h, 2 * h + 2))

                if not last:
                    y_bias(AT_Y1 + 1, 3, 1, 3 * i + 3)
                    gate(2, 2, 2)
                else:
                    gate(2, 1, 2)
                    y_bias(AT_Y1 + 1, 3, 1, 3 * i + 3)
                statistics(0)
                if last:
                    dve.wait_ge(last_gw_made, 1)
                centre((0, 1))
                if not last:
                    statistics(1)
                    centre((2, 3))
                    finish((0, 1), 1, 1)
                    finish((2, 3), 2, 2)
                else:
                    gate(3, 1, 3)
                    finish((0, 1), 1, 1)
                    statistics(1)
                    centre((2, 3))
                    finish((2,), 2, 2)
                    finish((3,), 2, 3)

            batch(0, first=True)
            with dve.Fori(1, B - 1) as i:
                batch(i)
            batch(B - 1, last=True)

        @block.tensor
        def _(pe):
            def claim(i, at, first=False):
                read, per_batch, count = reading_of((at - BANKS) % FILLS)
                if at >= BANKS:
                    pe.wait_ge(read, per_batch * i + count)
                elif not first:
                    pe.wait_ge(read, per_batch * (i - 1) + count)
                return bank[at % BANKS]

            def transpose_x0():
                for t in range(TT):
                    pe.wait_ge(xn_made, t + 1)
                    for k in range(CK):
                        last = nc.tensor.transpose(bank[AT_X0 + k][:, t * P:(t + 1) * P],
                                                   xn[:, t, k * P:(k + 1) * P], ident[:])
                        if t == TT - 1:
                            last.then_inc(xT_summed, 1)

            pe.wait_ge(consts_made, 4)
            for _ in range(WARM_UP):
                nc.tensor.matmul(bank[7][:, 0:P], ones[:], ident[:], start=True, stop=True)

            def split_product(dst, pairs, before_low=None):
                for n, (a, b) in enumerate(pairs):
                    if before_low and n == len(pairs) - CK:
                        pe.wait_ge(*before_low)
                    last = nc.tensor.matmul(dst, a, b, start=(n == 0), stop=(n == len(pairs) - 1))
                return last

            w2qT, w2kT = raw_qkv[:, 3], raw_qkv[:, 4]
            b2q, b2k = col[:, COL_B2:COL_B2 + CK], col[:, COL_B2 + CK:COL_B2 + 2 * CK]

            def fold_weights():
                for n in (3, 4):
                    pe.wait_ge(qkv_loaded[n], 16)
                for n in range(CK):
                    last = split_product(bank[6][:, n * C:(n + 1) * C],
                                         [(w2kT[:, k, n * P:(n + 1) * P], w2qT[:, k]) for k in range(CK)])
                last.then_inc(folded, 1)

            def fold_biases():
                pe.wait_ge(cols_loaded, 16)
                for n in range(CK):
                    split_product(FOLD_DW[:, n:n + 1], [(w2kT[:, k, n * P:(n + 1) * P], b2q[:, k:k + 1])
                                                        for k in range(CK)])
                    split_product(FOLD_Z[:, n:n + 1], [(w2qT[:, k, n * P:(n + 1) * P], b2k[:, k:k + 1])
                                                       for k in range(CK)])
                split_product(FOLD_D, [(b2q[:, k:k + 1].broadcast_to((P, P)), b2k[:, k:k + 1])
                                       for k in range(CK)]).then_inc(folded, 1)

            def sum_partitions(n):
                pe.wait_ge(abs_summed, n + 1)
                nc.tensor.matmul(GAMMA[n], ones[:], abs_sum[:, n:n + 1], start=True, stop=True).then_inc(gamma_summed, 1)

            def ffn_out(i, at, tiles):
                dst = claim(i, at)
                for n, t in enumerate(tiles):
                    last = split_product(dst[:, n * C:(n + 1) * C],
                                         [(r[part][:, f, t * P:(t + 1) * P], w2q[:, f])
                                          for part in ("lo", "hi") for f in range(FT)])
                last.then_inc(y_summed, 1)

            def batch(i, first=False):
                pe.wait_ge(xT_hi_made, 2 * i + 2)
                for m in range(6):
                    if first:
                        pe.wait_ge(w_split, m // 2 + 1)
                    dst = claim(i, AT_L1 + m, first)
                    h = slice((m % 2) * P, (m % 2 + 1) * P)
                    split_product(dst[:], [(w[a][:, m // 2, k, h], xT[b][:, k])
                                           for a, b in FULL for k in range(CK)],
                                  (xT_split, 2 * i + 2) if m == 0 else None).then_inc(l1_summed, 1)
                    if first and m == 1:
                        sum_partitions(0)
                    if first and m == 3:
                        pe.wait_ge(thr_made, 2)
                if first:
                    pe.wait_ge(fold_read, 2)
                    pe.wait_ge(w1_quantized, 2)
                for f in range(FT):
                    if first and f == 4:
                        pe.wait_ge(l1_read, 6)
                        sum_partitions(1)
                    if first and f == 7:
                        pe.wait_ge(thr_made, 4)
                    dst = claim(i, AT_F1 + f, first)
                    split_product(dst[:], [(w1q[:, k, f * P:(f + 1) * P], xT[part][:, k])
                                           for part in ("lo", "hi") for k in range(CK)]).then_inc(f1_summed, 1)
                pe.wait_ge(g_split, 6 * i + 4)
                for n in range(CK):
                    dst = claim(i, AT_K + n)
                    h = slice(n * P, (n + 1) * P)
                    split_product(dst[:], [(w[a][:, 3, k, h], g[b][:, 2 + k])
                                           for a, b in FULL for k in range(CK)]).then_inc(z_summed, 1)
                pe.wait_ge(g_split, 6 * i + 6)
                if first:
                    pe.wait_ge(w2v_split, 1)
                for n in range(2):
                    dst = claim(i, AT_V + n)
                    for t in (2 * n, 2 * n + 1):
                        done = split_product(dst[:, (t % 2) * C:(t % 2 + 1) * C],
                                             [(g[a][:, 4 + k, t * P:(t + 1) * P], w[b][:, 4, k])
                                              for a, b in FULL for k in range(CK)])
                    done.then_inc(v_summed, 1)
                if first:
                    pe.wait_ge(ones_rounded, 1)
                pe.wait_ge(e_split, i + 1)
                split_product(claim(i, AT_D)[:], [(ones_r[:], e[part][:]) for part in ("lo", "hi")]).then_inc(d_summed, 1)
                pe.wait_ge(r_split, 8 * i + 8)
                if first:
                    pe.wait_ge(w2_quantized, 2)
                ffn_out(i, AT_Y0, (0, 1))
                pe.wait_ge(z_split, 2 * i + 2)
                for j in range(TT):
                    dst = claim(i, AT_S + j)
                    split_product(dst[:, 0:S_COLS[j]], [(z[a][:, k, j * P:(j + 1) * P], g[b][:, k, j * P:T])
                                                        for a, b in FULL for k in range(CK)]).then_inc(s_summed, 1)
                ffn_out(i, AT_Y1, (2,))
                ffn_out(i, AT_Y1 + 1, (3,))
                pe.wait_ge(v_split, i + 1)
                for t in range(TT):
                    pe.wait_ge(s_split, 4 * i + t + 1)
                    dst = claim(i, AT_O + t)
                    split_product(dst[:, 0:C], [(s[a][:, S_AT[j] + (t - j) * P:S_AT[j] + (t - j + 1) * P], v[b][:, j])
                                                for a, b in FULL for j in range(t + 1)]).then_inc(o_summed, 1)

            fold_weights()
            transpose_x0()
            fold_biases()
            batch(0, first=True)
            with pe.Fori(1, B) as i:
                batch(i)


def kernel(**inputs):
    import numpy as np
    import concourse.bacc as bacc
    from concourse.bass_utils import run_bass_kernel_spmd

    def by_partition(name):
        return np.asarray(inputs[name]).reshape(-1, P).T

    arrays = {"x": np.ascontiguousarray(inputs["L0_attn_x"]),
              "x_t": np.ascontiguousarray(np.swapaxes(inputs["L0_attn_x"], 1, 2))}
    for name in ("W1q", "W1k", "W1v", "W2v"):
        arrays[name] = np.ascontiguousarray(inputs["L0_attn_" + name])
    for name in ("W2q", "W2k"):
        arrays[name] = np.ascontiguousarray(np.asarray(inputs["L0_attn_" + name]).T)
    arrays["w1t"] = np.ascontiguousarray(np.asarray(inputs["L0_ffn_W1"]).T)
    arrays["w2t"] = np.ascontiguousarray(np.asarray(inputs["L0_ffn_W2"]).T)
    arrays["cols"] = np.ascontiguousarray(np.concatenate(
        [by_partition(n) for n in ("L0_attn_b1q", "L0_attn_b1k", "L0_attn_b1v", "L0_attn_b2q", "L0_attn_b2k",
                                   "L0_ffn_b1")], axis=1))
    arrays["rows"] = np.ascontiguousarray(np.stack(
        [np.asarray(inputs[n]) for n in ("L0_attn_b2v", "L0_ffn_b2", "L0_attn_ln_w", "L0_attn_ln_b")]))

    nc = bacc.Bacc("TRN2", target_bir_lowering=False, num_devices=1, dynamic_dma_scratch_size=1024)
    aps = {n: nc.dram_tensor(f"in_{n}", a.shape, FP32, kind="ExternalInput").ap() for n, a in arrays.items()}
    out = nc.dram_tensor("out", (B, T, C), FP32, kind="ExternalOutput").ap()
    x_norm_rows = nc.dram_tensor("x_norm_rows", (B, P, 2, TT), FP32, kind="Internal").ap()
    gated_block(nc, aps["x"], aps["x_t"], x_norm_rows, [aps[n] for n in ("W1q", "W1k", "W1v", "W2q", "W2k", "W2v")],
                aps["w1t"], aps["w2t"], aps["cols"], aps["rows"], out)
    result = run_bass_kernel_spmd(nc, [{f"in_{n}": a for n, a in arrays.items()}], core_ids=[0])
    return result.results[0]["out"]
```
